# Optimizing a Trainium2 kernel written in Bass

```python
import numpy as np
import jax
import jax.numpy as jnp

def _softmax(x, axis=-1):
    return jax.nn.softmax(x, axis=axis)

def _gelu(x):
    return jax.nn.gelu(x, approximate=True)

def _silu(x):
    return jax.nn.silu(x)

def _sigmoid(x):
    return jax.nn.sigmoid(x)

def _layernorm(x, axis=-1, eps=1e-05):
    m = jnp.mean(x, axis=axis, keepdims=True)
    v = jnp.var(x, axis=axis, keepdims=True)
    return (x - m) / jnp.sqrt(v + eps)

def _scatter_add(tgt, idx, src, axis=0):
    return tgt.at[idx].add(src)

def _segment_sum(src, seg, n):
    return jax.ops.segment_sum(src, seg, n)
kernel_name = 'mk_adaln_ffn_d1_seqx_r8_44cdf5'

def setup_inputs(seed: int=0):
    np.random.seed(seed)
    _w = jnp.asarray

    def _rec_inputs():
        import jax
        import jax.numpy as jnp
        _rk = jax.random.key(seed)
        x = -0.000125 + 0.9999 * jax.random.normal(jax.random.fold_in(_rk, 1), (32, 128, 128), jnp.float32)
        _lenS = 128 - jax.random.randint(jax.random.fold_in(_rk, 7), (32,), 0, max(1, 128 // 4) + 1, jnp.int32)
        _lenS2 = 128 - jax.random.randint(jax.random.fold_in(_rk, 8), (32,), 0, max(1, 128 // 4) + 1, jnp.int32)
        itok_B_0_15 = jax.random.randint(jax.random.fold_in(_rk, 11), (32,), 0, 16, jnp.int32)
        return (x, itok_B_0_15)
    x, itok_B_0_15 = _rec_inputs()

    def _L0_cond_setup():
        import jax, jax.numpy as jnp
        import numpy as np
        B, N, DIM = (32, 128, 128)
        HID = 512
        PART = 32
        OUT = 128
        SHARED = OUT - PART
        E = 16
        key = jax.random.key(seed)
        ks = jax.random.split(key, 8)
        s = 0.02
        return {'x': jax.random.normal(ks[0], (B, N, DIM), dtype=jnp.float32), 'indices': jax.random.randint(ks[1], (B,), 0, E, dtype=jnp.int64), 'fc1_w': jax.random.normal(ks[2], (HID, DIM), dtype=jnp.float32) * s, 'fc1_b': jnp.zeros((HID,), dtype=jnp.float32), 'fc2_w': jax.random.normal(ks[3], (SHARED, HID), dtype=jnp.float32) * s, 'fc2_b': jnp.zeros((SHARED,), dtype=jnp.float32), 'experts_w': jax.random.normal(ks[4], (E, PART, HID), dtype=jnp.float32) * s, 'experts_b': jnp.zeros((E, PART), dtype=jnp.float32)}
    _L0_cond_all = _L0_cond_setup()
    _L0_cond_in = {k: v for k, v in _L0_cond_all.items() if k in ('fc1_w', 'fc1_b', 'fc2_w', 'fc2_b', 'experts_w', 'experts_b')}
    del _L0_cond_all

    def _L0_ffn_setup():
        import jax, jax.numpy as jnp
        import numpy as np
        HIDDEN = 128
        NUM_EXPERTS = 8
        TOP_K = 2
        FFN = 512
        BATCH, SEQ = (4, 256)
        key = jax.random.key(seed)
        k_x, k_r, k_w1, k_w2 = jax.random.split(key, 4)
        x = jax.random.normal(k_x, (BATCH, SEQ, HIDDEN), dtype=jnp.float32)
        router_w = jax.random.normal(k_r, (NUM_EXPERTS, HIDDEN), dtype=jnp.float32) * (1.0 / np.sqrt(HIDDEN))
        lim = float(np.sqrt(6.0 / (FFN + HIDDEN)))
        expert_w1 = jax.random.uniform(k_w1, (NUM_EXPERTS, FFN, HIDDEN), dtype=jnp.float32, minval=-lim, maxval=lim)
        expert_w2 = jax.random.uniform(k_w2, (NUM_EXPERTS, HIDDEN, FFN), dtype=jnp.float32, minval=-lim, maxval=lim)
        return {'x': x, 'router_w': router_w, 'expert_w1': expert_w1, 'expert_w2': expert_w2}
    _L0_ffn_all = _L0_ffn_setup()
    _L0_ffn_in = {k: v for k, v in _L0_ffn_all.items() if k in ('router_w', 'expert_w1', 'expert_w2')}
    del _L0_ffn_all
    return {'x': x, 'itok_B_0_15': itok_B_0_15, 'L0_cond_fc1_w': _L0_cond_in['fc1_w'], 'L0_cond_fc1_b': _L0_cond_in['fc1_b'], 'L0_cond_fc2_w': _L0_cond_in['fc2_w'], 'L0_cond_fc2_b': _L0_cond_in['fc2_b'], 'L0_cond_experts_w': _L0_cond_in['experts_w'], 'L0_cond_experts_b': _L0_cond_in['experts_b'], 'L0_ffn_router_w': _L0_ffn_in['router_w'], 'L0_ffn_expert_w1': _L0_ffn_in['expert_w1'], 'L0_ffn_expert_w2': _L0_ffn_in['expert_w2']}

def reference(x, itok_B_0_15, L0_cond_fc1_w, L0_cond_fc1_b, L0_cond_fc2_w, L0_cond_fc2_b, L0_cond_experts_w, L0_cond_experts_b, L0_ffn_router_w, L0_ffn_expert_w1, L0_ffn_expert_w2):
    import jax
    import jax.numpy as jnp

    def _L0_cond_ref(x, indices, fc1_w, fc1_b, fc2_w, fc2_b, experts_w, experts_b):
        import jax, jax.numpy as jnp
        import numpy as np
        B, N, DIM = (32, 128, 128)
        HID = 512
        PART = 32
        OUT = 128
        SHARED = OUT - PART
        E = 16
        h = jax.nn.gelu(jnp.einsum('bnd,hd->bnh', x, fc1_w) + fc1_b, approximate=False)
        shared = jnp.einsum('bnh,sh->bns', h, fc2_w) + fc2_b
        We = experts_w[indices]
        be = experts_b[indices]
        expert_x = jnp.einsum('bnh,bph->bnp', h, We) + be[:, None, :]
        return jnp.concatenate([shared, expert_x], axis=-1)

    def _L0_ffn_ref(x, router_w, expert_w1, expert_w2):
        import jax, jax.numpy as jnp
        import numpy as np
        HIDDEN = 128
        NUM_EXPERTS = 8
        TOP_K = 2
        FFN = 512
        BATCH, SEQ = (4, 256)
        B, S, D = x.shape
        xf = x.reshape(-1, D)
        scores = xf @ router_w.T
        top_v, top_i = jax.lax.top_k(scores, TOP_K)
        routing_w = jax.nn.softmax(top_v, axis=-1)
        out = jnp.zeros_like(xf)
        for e in range(NUM_EXPERTS):
            w_e = jnp.sum(jnp.where(top_i == e, routing_w, 0.0), axis=-1)
            h = jax.nn.gelu(xf @ expert_w1[e].T, approximate=False)
            out = out + h @ expert_w2[e].T * w_e[:, None]
        return out.reshape(B, S, D)
    x = x + _L0_ffn_ref(_L0_cond_ref(x, itok_B_0_15, L0_cond_fc1_w, L0_cond_fc1_b, L0_cond_fc2_w, L0_cond_fc2_b, L0_cond_experts_w, L0_cond_experts_b), L0_ffn_router_w, L0_ffn_expert_w1, L0_ffn_expert_w2)
    return x

_drawn_inputs = setup_inputs


def setup_inputs(seed=0):
    import zlib

    import numpy as np

    out = dict(_drawn_inputs(seed))
    spreads = {'L0_cond_fc1_b': (0.0, 0.363),
     'L0_cond_fc2_b': (0.0, 0.297),
     'L0_cond_experts_b': (0.0, 0.307)}
    factors = {'L0_cond_experts_w': 3.286}
    for name, (base, spread) in spreads.items():
        noise = np.random.default_rng([zlib.crc32(name.encode()), seed]).standard_normal(out[name].shape)
        drawn = base * np.exp(spread * noise) if base else spread * noise
        out[name] = jnp.asarray(drawn.astype(out[name].dtype))
    for name, factor in factors.items():
        out[name] = (out[name] * factor).astype(out[name].dtype)
    return out
```

```python
from contextlib import ExitStack

import concourse.bass as bass
from concourse import mybir

F32 = mybir.dt.float32
F32R = mybir.dt.float32r
F16 = mybir.dt.float16
BF16 = mybir.dt.bfloat16
I32 = mybir.dt.int32
ALU = mybir.AluOpType
ACT = mybir.ActivationFunctionType
AX = mybir.AxisListType.X

P = 128
SEQS = 32
TOKENS = SEQS * P
HID = 512
FB = HID // P
GB = FB // 2
PART = 32
SHARED = P - PART
CEXP = 16
EXP = 8
TOPK = 2
TILE = 512
RPT = TILE // P
CHUNKS = TOKENS // TILE
PAIRS = TOPK * SEQS
TILES = (TOPK * TOKENS + EXP * (TILE - 1)) // TILE
BLOCKS = TILES * RPT
LAG = 2
MAXT = 8
TOKEN_SHIFT = TOKENS // 2
LIST_GROUP = 4
FIN_GROUP = 4
NEG = -3.0e38


class Step:

    def __init__(self, pair, offset):
        self.pair, self.offset = pair, offset
        self.value = 2 * pair + offset
        self.parity = offset % 2
        self.half = pair + offset // 2

    def __add__(self, d):
        return Step(self.pair, self.offset + d)

    def __sub__(self, d):
        return self + (-d)

    def within(self, n):
        return not isinstance(self.value, int) or 0 <= self.value < n


def wait(eng, sem, value):
    if not isinstance(value, int) or value > 0:
        eng.wait_ge(sem, value)


def run_steps(eng, n, body):
    pairs = (n - 1 - LAG) // 2
    for s in range(LAG):
        body(Step(0, s))
    with eng.Fori(1, 1 + pairs) as i:
        body(Step(i, 0))
        body(Step(i, 1))
    for s in range(LAG + 2 * pairs, n + LAG):
        body(Step(s // 2, s % 2))


def run_pairs(eng, n, body):
    body(Step(0, 0))
    body(Step(0, 1))
    with eng.Fori(1, n // 2) as i:
        body(Step(i, 0))
        body(Step(i, 1))
    if n % 2:
        body(Step(n // 2, 0))


def build(nc, xT, x, itok, fc1T, fc1_b, fc2T, fc2_b, cexpT, cexp_b, routerT, w1T, w2T, out):
    assert LAG == 2
    y_rows = nc.dram_tensor("y_rows", (TOKENS, P), F32, kind="Internal").ap()
    z_rows = nc.dram_tensor("z_rows", (TILES * TILE, P), F32, kind="Internal").ap()
    y_store = y_rows.rearrange("(c r p) d -> p c r d", r=RPT, p=P)
    z_store = z_rows.rearrange("(c r p) d -> p c r d", r=RPT, p=P)
    x_all = x.rearrange("s p d -> p s d")
    out_store = out.rearrange("s p d -> p s d")

    with ExitStack() as ctx:
        def sb(name, shape, dt=F32):
            return ctx.enter_context(nc.sbuf_tensor(name, shape, dt))

        def ps(name, shape):
            return ctx.enter_context(nc.psum_tensor(name, shape, F32))

        def sem(name):
            return ctx.enter_context(nc.semaphore(name))

        fc1_raw = sb("fc1_raw", [P, HID])
        fc1 = sb("fc1", [P, 2, HID], F32R)
        fc2_raw = sb("fc2_raw", [P, FB, SHARED])
        fc2 = sb("fc2", [P, 2, FB, SHARED], F32R)
        cexp_raw = sb("cexp_raw", [P, 2, RPT, FB, PART])
        cexp = sb("cexp", [P, 2, 2, FB, RPT, PART], F32R)
        ffn_raw = sb("ffn_raw", [P, 2, 2 * HID])
        ffn = sb("ffn", [P, EXP, 2, 2, HID], F32R)
        w1 = sb("w1", [P, 2, 2, HID], F32R)
        w2 = sb("w2", [P, 2, 2, HID], F32R)
        router = sb("router", [P, EXP])
        fc1_bias = sb("fc1_bias", [P, FB])
        fc2_bias = sb("fc2_bias", [SHARED, 1])
        cexp_bias = sb("cexp_bias", [CEXP, PART])
        seq_bias = sb("seq_bias", [P, SEQS])
        x_raw = sb("x_raw", [P, 2, TILE])
        xs = sb("xs", [P, 2, 2, TILE], F32R)
        hid = sb("hid", [P, 2, GB * TILE])
        hs = sb("hs", [P, 2, 2, 2, GB * TILE], F32R)
        yT = sb("yT", [P, TILE])
        rows = sb("rows", [P, 2, RPT, P])
        picked = sb("picked", [P, 2, RPT, P])
        x_rows = sb("x_rows", [P, SEQS, P])
        ident = sb("ident", [P, P])
        ones_b = sb("ones_b", [P, P], BF16)
        before = sb("before", [P, P], BF16)
        lane_i = sb("lane_i", [P, P], I32)
        lane = sb("lane", [P, P], F16)
        part_i = sb("part_i", [CEXP, 1], I32)
        part_f = sb("part_f", [CEXP, 1])
        rank_i = sb("rank_i", [P, EXP], I32)
        rank = sb("rank", [P, EXP])
        fill_i = sb("fill_i", [P, MAXT], I32)
        fill = sb("fill", [P, MAXT])
        tile_i = sb("tile_i", [P, TILES], I32)
        tile_f = sb("tile_f", [P, TILES])
        tok_i = sb("tok_i", [P, SEQS, TOPK], I32)
        tok = sb("tok", [P, SEQS, TOPK])
        ones_f = sb("ones_f", [P, EXP * PAIRS])
        itok_row = sb("itok_row", [1, SEQS], I32)
        itok_all = sb("itok_all", [CEXP, SEQS], I32)
        itok_f = sb("itok_f", [CEXP, SEQS])
        seq_hot = sb("seq_hot", [CEXP, SEQS])
        score = sb("score", [P, SEQS, EXP])
        top = sb("top", [P, TOPK, SEQS])
        first = sb("first", [P, TOPK, SEQS])
        same = sb("same", [P, SEQS, EXP])
        same_r = sb("same_r", [P, SEQS, EXP])
        rest = sb("rest", [P, SEQS, EXP])
        chosen = sb("chosen", [P, SEQS, TOPK, EXP], BF16)
        gap = sb("gap", [P, SEQS])
        egap = sb("egap", [P, SEQS])
        denom = sb("denom", [P, SEQS])
        gate = sb("gate", [P, TOPK, SEQS])
        pair_e = [hid[:, n // 2, (n % 2) * TILE:(n % 2 + 1) * TILE] for n in range(4)]
        total, upto, start = (v.rearrange("p (e j) -> p e j", e=EXP) for v in pair_e[:3])
        place, place_m = (v.rearrange("p (j e) -> p j e", e=EXP) for v in (pair_e[3], pair_e[0]))
        count = sb("count", [P, EXP])
        over = sb("over", [P, EXP, MAXT])
        tiles = sb("tiles", [P, EXP])
        tiles_upto = sb("tiles_upto", [P, EXP])
        tiles_from = sb("tiles_from", [P, EXP])
        shift = sb("shift", [P, EXP])
        passed = sb("passed", [P, TILES, EXP])
        owner_f = sb("owner_f", [P, TILES])
        owner_i = sb("owner_i", [P, TILES], I32)
        slot = sb("slot", [P, PAIRS])
        slot_i = sb("slot_i", [P, PAIRS], I32)
        block_i = sb("block_i", [P, PAIRS], I32)
        block = sb("block", [P, PAIRS])
        line_i = sb("line_i", [P, PAIRS], I32)
        line = sb("line", [P, PAIRS])
        line_hot = sb("line_hot", [P, 2, LIST_GROUP, P], F16)
        block_tok = sb("block_tok", [P, 2, LIST_GROUP, BLOCKS], F16)
        source = sb("source", [P, BLOCKS], I32)
        source_now = sb("source_now", [P, 2, RPT], I32)
        slot_now = sb("slot_now", [P, 2, FIN_GROUP * TOPK], I32)

        hp = ps("hp", [P, 2, GB * TILE])
        dn = ps("dn", [P, TILE])
        dx = ps("dx", [P, TILE])
        tr = ps("tr", [P, RPT, P])
        misc = ps("misc", [P, TILE])

        s_const = sem("s_const")
        s_constf = sem("s_constf")
        s_load = [sem(f"s_load{n}") for n in range(9)]
        s_xrows = sem("s_xrows")
        s_xin = [sem(f"s_xin{n}") for n in range(2)]
        s_cexp = [sem(f"s_cexp{n}") for n in range(2)]
        s_ffn = [sem(f"s_ffn{n}") for n in range(2)]
        s_wprep_hi, s_wprep_lo = sem("s_wprep_hi"), sem("s_wprep_lo")
        s_fc_hi, s_fc_lo = sem("s_fc_hi"), sem("s_fc_lo")
        s_hot, s_bias, s_biasc = sem("s_hot"), sem("s_bias"), sem("s_biasc")
        s_chi, s_clo = sem("s_chi"), sem("s_clo")
        s_rows_out = [sem(f"s_rows_out{n}") for n in range(2)]
        s_chain = sem("s_chain")
        s_gap, s_exp = sem("s_gap"), sem("s_exp")
        s_chosen, s_rank = sem("s_chosen"), sem("s_rank")
        s_owner, s_line, s_listed = sem("s_owner"), sem("s_line"), sem("s_listed")
        s_source, s_slot = sem("s_source"), sem("s_slot")
        s_snow = sem("s_snow")
        s_go, s_sp_go = sem("s_go"), sem("s_sp_go")
        s_pick = [sem(f"s_pick{n}") for n in range(2)]
        s_w1 = [sem(f"s_w1{n}") for n in range(2)]
        s_w2 = [sem(f"s_w2{n}") for n in range(2)]
        s_zout = [sem(f"s_zout{n}") for n in range(2)]
        s_znow = sem("s_znow")
        s_back = [sem(f"s_back{n}") for n in range(2)]
        s_half, s_fin = sem("s_half"), sem("s_fin")
        s_out = [sem(f"s_out{n}") for n in range(2)]

        class Counts:

            def __init__(self, tag, per_group):
                self.per = per_group
                self.xhi = sem(tag + "xhi")
                self.xlo = sem(tag + "xlo")
                self.up = sem(tag + "up")
                self.gelu = sem(tag + "gelu")
                self.hi = sem(tag + "hi")
                self.lo = sem(tag + "lo")
                self.down = sem(tag + "down")
                self.flat = sem(tag + "flat")
                self.turned = sem(tag + "turned")
                self.rows = sem(tag + "rows")
                self.tin = sem(tag + "tin")
                self.score = sem(tag + "score")

        A, C = Counts("a_", GB), Counts("c_", 1)

        def pe_up(pe, k, st, g, weight):
            wait(pe, k.gelu, 2 * k.per * (st.value - 1) + k.per * (g + 1))
            for n in range(GB):
                cols = slice((g * GB + n) * P, (g * GB + n + 1) * P)
                dst = hp[:, g, n * TILE:(n + 1) * TILE]
                passes = [(0, 1), (1, 0), (0, 0)]
                for m, (w, v) in enumerate(passes):
                    mm = pe.matmul(dst, weight[:, w, cols], xs[:, st.parity, v, :],
                                   start=m == 0, stop=m == len(passes) - 1)
                if k.per == GB or n == GB - 1:
                    mm.then_inc(k.up, 1)

        def pe_down(pe, k, st, g, products, last_inc):
            wait(pe, k.lo, 2 * st.value + g + 1)
            for dst, weight in products:
                for n in range(GB):
                    f = g * GB + n
                    for m, (w, v) in enumerate([(0, 1), (1, 0), (0, 0)]):
                        mm = pe.matmul(dst, weight(w, f), hs[:, st.parity, v, g, n * TILE:(n + 1) * TILE],
                                       start=(f == 0 and m == 0), stop=(f == FB - 1 and m == 2))
            if last_inc:
                mm.then_inc(k.down, 1)

        def act_hidden(act, k, st, g, bias):
            wait(act, k.lo, 2 * (st.value - 1) + g + 1)
            n_per = GB // k.per
            for n in range(k.per):
                wait(act, k.up, 2 * k.per * st.value + k.per * g + n + 1)
                cols = slice(n * n_per * TILE, (n + 1) * n_per * TILE)
                if bias is None:
                    ins = act.activation(hid[:, g, cols], hp[:, g, cols], ACT.Gelu)
                else:
                    f = g * GB + n
                    ins = act.activation(hid[:, g, cols], hp[:, g, cols], ACT.Gelu, bias=bias[:, f:f + 1])
                ins.then_inc(k.gelu, 1)
            wait(act, k.gelu, 2 * k.per * st.value + k.per * (g + 1))
            wait(act, k.down, st.value - 1)
            act.activation(hs[:, st.parity, 0, g, :], hid[:, g, :], ACT.Copy).then_inc(k.hi, 1)

        def dve_hidden(dve, k, st, g):
            wait(dve, k.hi, 2 * st.value + g + 1)
            dve.tensor_tensor(hs[:, st.parity, 1, g, :], hid[:, g, :],
                              hs[:, st.parity, 0, g, :].bitcast(F32), ALU.subtract).then_inc(k.lo, 1)

        block_ctx = ctx.enter_context(nc.Block())

        @block_ctx.sync
        def _(sp):
            sp.dma_start(itok_row[:, :], itok).then_inc(s_load[0], 16)
            sp.dma_start(x_raw[:, 0, :], xT[:, 0:TILE]).then_inc(s_xin[0], 16)
            sp.dma_start(fc1_raw[:, :], fc1T).then_inc(s_load[1], 16)
            sp.dma_start(fc1_bias[:, :], fc1_b).then_inc(s_load[2], 16)
            sp.dma_start(fc2_raw[:, :, :], fc2T).then_inc(s_load[3], 16)
            sp.dma_start(fc2_bias[:, :], fc2_b).then_inc(s_load[4], 16)
            sp.dma_start(itok_all[:, :], itok.to_broadcast((CEXP, SEQS))).then_inc(s_load[5], 16)
            sp.dma_start(cexp_bias[:, :], cexp_b).then_inc(s_load[6], 16)
            sp.dma_start(router[:, :], routerT).then_inc(s_load[7], 16)

            def load_chunk(st):
                c, u = st.value, st.parity
                if not isinstance(c, int) or c > 0:
                    wait(sp, A.xlo, c - 1)
                    sp.dma_start(x_raw[:, u, :], xT[:, bass.ds(c * TILE, TILE)]).then_inc(s_xin[u], 16)
                wait(sp, s_clo, c - 1)
                sp.wait_ge(s_load[0], 16)
                sp.sem_inc(s_sp_go, 1)
                for r in range(RPT):
                    e = sp.value_load(itok_row[0:1, bass.ds(c * RPT + r, 1)], min_val=0, max_val=CEXP - 1)
                    sp.dma_start(cexp_raw[:, u, r, :, :].rearrange("p f c -> p (f c)"),
                                 cexpT[bass.ds(e, 1), :, :].rearrange("e p n -> p (e n)"))\
                      .then_inc(s_cexp[u], 16)
                wait(sp, s_wprep_lo, c - 1)
                sp.dma_start(ffn_raw[:, u, 0:HID], w1T[:, bass.ds(c, 1), :].rearrange("p e n -> p (e n)"))\
                  .then_inc(s_ffn[u], 16)
                sp.dma_start(ffn_raw[:, u, HID:2 * HID], w2T[:, bass.ds(c, 1), :].rearrange("p e n -> p (e n)"))\
                  .then_inc(s_ffn[u], 16)

            def step_a(st):
                if (st + 1).within(CHUNKS):
                    load_chunk(st + 1)
                if (st - 2).within(CHUNKS):
                    done = st - 2
                    wait(sp, A.rows, done.value + 1)
                    sp.dma_start(y_store[:, bass.ds(done.value, 1), :, :].rearrange("p c r d -> p (c r) d"),
                                 rows[:, done.parity, :, :]).then_inc(s_rows_out[done.parity], 16)

            load_chunk(Step(0, 0))
            run_steps(sp, CHUNKS, step_a)
            sp.dma_start(x_rows[:, :, :], x_all).then_inc(s_xrows, 16)

            def load_weights(st, which, dst, sems):
                sp.sem_inc(s_sp_go, 1)
                e = sp.value_load(owner_i[0:1, bass.ds(st.value, 1)], min_val=0, max_val=EXP - 1)
                sp.dma_start(dst[:, st.parity, :, :].rearrange("p h n -> p (h n)").bitcast(F32),
                             ffn[:, bass.ds(e, 1), which, :, :].rearrange("p e h n -> p (e h n)").bitcast(F32))\
                  .then_inc(sems[st.parity], 16)

            def step_c(st):
                if (st + 1).within(TILES):
                    wait(sp, C.up, 2 * st.value)
                    load_weights(st + 1, 0, w1, s_w1)
                if st.within(TILES):
                    wait(sp, C.down, st.value - 1)
                    load_weights(st, 1, w2, s_w2)
                if (st - 2).within(TILES):
                    done = st - 2
                    wait(sp, C.rows, done.value + 1)
                    sp.dma_start(z_store[:, bass.ds(done.value, 1), :, :].rearrange("p c r d -> p (c r) d"),
                                 rows[:, done.parity, :, :]).then_inc(s_zout[done.parity], 16)

            sp.wait_ge(s_owner, 1)
            sp.wait_ge(s_wprep_lo, EXP)
            load_weights(Step(0, 0), 0, w1, s_w1)
            run_steps(sp, TILES, step_c)

            def store_out(st):
                wait(sp, s_fin, st.value + 1)
                sp.dma_start(out_store[:, bass.ds(st.value * FIN_GROUP, FIN_GROUP), :],
                             rows[:, st.parity, :, :]).then_inc(s_out[st.parity], 16)

            with sp.Fori(0, SEQS // FIN_GROUP // 2) as i:
                store_out(Step(i, 0))
                store_out(Step(i, 1))
            for u in range(2):
                sp.wait_ge(s_out[u], 16 * (SEQS // FIN_GROUP // 2))

        @block_ctx.gpsimd
        def _(pool):
            pool.memset(ident[:, :], 1.0).then_inc(s_const, 1)
            pool.memset(before[:, :], 1.0).then_inc(s_const, 1)
            pool.memset(ones_b[:, :], 1.0).then_inc(s_const, 1)
            pool.memset(ones_f[:, :], 1.0).then_inc(s_const, 1)
            pool.iota(part_i[:, :], [[0, 1]], base=0, channel_multiplier=1).then_inc(s_const, 1)
            pool.iota(lane_i[:, :], [[1, P]], base=0, channel_multiplier=0).then_inc(s_const, 1)
            pool.iota(rank_i[:, :], [[-1, EXP]], base=EXP, channel_multiplier=0).then_inc(s_const, 1)
            pool.iota(fill_i[:, :], [[TILE, MAXT]], base=0, channel_multiplier=0).then_inc(s_const, 1)
            pool.iota(tile_i[:, :], [[1, TILES]], base=0, channel_multiplier=0).then_inc(s_const, 1)
            pool.iota(tok_i[:, :, :], [[P, SEQS], [0, TOPK]], base=-TOKEN_SHIFT, channel_multiplier=1)\
                .then_inc(s_const, 1)
            pool.wait_ge(s_const, 10)
            pool.affine_select(out=ident[:, :], in_=ident[:, :], compare_op=ALU.is_equal, fill=0.0,
                               base=0, pattern=[[-1, P]], channel_multiplier=1).then_inc(s_const, 1)
            pool.affine_select(out=before[:, :], in_=before[:, :], compare_op=ALU.is_gt, fill=0.0,
                               base=0, pattern=[[1, P]], channel_multiplier=-1).then_inc(s_const, 1)

            def split_expert(st):
                wait(pool, s_ffn[st.parity], 32 * st.half + 32)
                pair = ffn_raw[:, st.parity, :].rearrange("p (w n) -> p w n", w=2)
                hi = ffn[:, bass.ds(st.value, 1), :, 0, :].rearrange("p e w n -> p (e w) n")
                lo = ffn[:, bass.ds(st.value, 1), :, 1, :].rearrange("p e w n -> p (e w) n")
                pool.tensor_copy(hi, pair).then_inc(s_wprep_hi, 1)
                wait(pool, s_wprep_hi, st.value + 1)
                pool.tensor_tensor(lo, pair, hi.bitcast(F32), ALU.subtract).then_inc(s_wprep_lo, 1)

            with pool.Fori(0, EXP // 2) as i:
                split_expert(Step(i, 0))
                split_expert(Step(i, 1))

            pool.wait_ge(s_source, 1)
            for u in range(2):
                pool.wait_ge(s_rows_out[u], 16 * (1 + CHUNKS // 2))

            def gather_tile(st):
                t, u = st.value, st.parity
                wait(pool, s_pick[u], 16 * RPT * st.half)
                pool.tensor_copy(source_now[:, u, :], source[:, bass.ds(t * RPT, RPT)]).then_inc(s_snow, 1)
                wait(pool, s_snow, t + 1)
                wait(pool, C.tin, t - 1)
                pool.sem_inc(s_go, 1)
                for r in range(RPT):
                    pool.indirect_dma_start(
                        out=picked[:, u, r, :], out_offset=None, in_=y_rows,
                        in_offset=bass.IndirectOffsetOnAxis(ap=source_now[:, u, r:r + 1], axis=0))\
                        .then_inc(s_pick[u], 16)

            run_pairs(pool, TILES, gather_tile)

            pool.wait_ge(s_slot, 1)
            for u in range(2):
                pool.wait_ge(s_zout[u], 16 * (1 + (TILES + 1 - u) // 2))

            def gather_back(st):
                t, u, n = st.value, st.parity, FIN_GROUP * TOPK
                wait(pool, s_back[u], 16 * n * st.half)
                pool.tensor_copy(slot_now[:, u, :], slot_i[:, bass.ds(t * n, n)]).then_inc(s_znow, 1)
                wait(pool, s_znow, t + 1)
                wait(pool, s_fin, t - 1)
                pool.sem_inc(s_go, 1)
                for r in range(n):
                    pool.indirect_dma_start(
                        out=hid[:, u, r * P:(r + 1) * P], out_offset=None, in_=z_rows,
                        in_offset=bass.IndirectOffsetOnAxis(ap=slot_now[:, u, r:r + 1], axis=0))\
                        .then_inc(s_back[u], 16)

            run_pairs(pool, SEQS // FIN_GROUP, gather_back)

        @block_ctx.scalar
        def _(act):
            act.wait_ge(s_load[1], 16)
            act.activation(fc1[:, 0, :], fc1_raw[:, :], ACT.Copy).then_inc(s_fc_hi, 1)

            def split_x(st):
                wait(act, s_xin[st.parity], 16 * st.half + 16)
                act.activation(xs[:, st.parity, 0, :], x_raw[:, st.parity, :], ACT.Copy).then_inc(A.xhi, 1)

            split_x(Step(0, 0))
            act.wait_ge(s_load[3], 16)
            act.activation(fc2[:, 0, :, :], fc2_raw[:, :, :], ACT.Copy).then_inc(s_fc_hi, 1)
            act.wait_ge(s_load[2], 16)

            def step_a(st):
                if st.within(CHUNKS):
                    act_hidden(act, A, st, 0, fc1_bias)
                    if (st + 1).within(CHUNKS):
                        split_x(st + 1)
                    wait(act, s_cexp[st.parity], 16 * RPT * (st.half + 1))
                    act.activation(cexp[:, st.parity, 0, :, :, :],
                                   cexp_raw[:, st.parity, :, :, :].rearrange("p r f c -> p f r c"),
                                   ACT.Copy).then_inc(s_chi, 1)
                    act_hidden(act, A, st, 1, fc1_bias)

            run_steps(act, CHUNKS, step_a)

            act.wait_ge(s_gap, 1)
            act.activation(egap[:, :], gap[:, :], ACT.Exp).then_inc(s_exp, 1)

            def split_picked(st):
                wait(act, C.tin, st.value + 1)
                act.activation(xs[:, st.parity, 0, :], dx[:, :], ACT.Copy).then_inc(C.xhi, 1)

            def step_c(st):
                if st.within(TILES):
                    act_hidden(act, C, st, 0, None)
                    if (st + 1).within(TILES):
                        split_picked(st + 1)
                    act_hidden(act, C, st, 1, None)

            split_picked(Step(0, 0))
            run_steps(act, TILES, step_c)

        @block_ctx.vector
        def _(dve):
            links = [0]

            def link(ins):
                links[0] += 1
                ins.then_inc(s_chain, 1)
                dve.wait_ge(s_chain, links[0])

            for u in range(2):
                dve.sem_inc(s_rows_out[u], 16)
                dve.sem_inc(s_zout[u], 16)
            dve.wait_ge(s_fc_hi, 1)
            dve.tensor_tensor(fc1[:, 1, :], fc1_raw[:, :], fc1[:, 0, :].bitcast(F32), ALU.subtract)\
               .then_inc(s_fc_lo, 1)

            def split_x(st):
                wait(dve, A.xhi, st.value + 1)
                dve.tensor_tensor(xs[:, st.parity, 1, :], x_raw[:, st.parity, :],
                                  xs[:, st.parity, 0, :].bitcast(F32), ALU.subtract).then_inc(A.xlo, 1)

            split_x(Step(0, 0))
            dve.wait_ge(s_const, 12)
            dve.tensor_copy(part_f[:, :], part_i[:, :])
            dve.tensor_copy(lane[:, :], lane_i[:, :])
            dve.tensor_copy(rank[:, :], rank_i[:, :])
            dve.tensor_copy(fill[:, :], fill_i[:, :])
            dve.tensor_copy(tile_f[:, :], tile_i[:, :])
            dve.tensor_copy(tok[:, :, :], tok_i[:, :, :])
            dve.wait_ge(s_load[5], 16)
            link(dve.tensor_copy(itok_f[:, :], itok_all[:, :]))
            dve.tensor_scalar(seq_hot[:, :], itok_f[:, :], part_f[:, 0:1], None, ALU.is_equal)\
               .then_inc(s_hot, 1)
            dve.wait_ge(s_fc_hi, 2)
            dve.tensor_tensor(fc2[:, 1, :, :], fc2_raw[:, :, :], fc2[:, 0, :, :].bitcast(F32), ALU.subtract)\
               .then_inc(s_fc_lo, 1)
            dve.wait_ge(s_bias, 1)
            dve.tensor_copy(seq_bias[SHARED:P, :], misc[SHARED:P, 0:SEQS]).then_inc(s_biasc, 1)
            dve.wait_ge(s_biasc, 1)
            dve.wait_ge(s_load[4], 16)

            def step_a(st):
                if (st - 2).within(CHUNKS):
                    done = st - 2
                    wait(dve, A.turned, done.value + 1)
                    wait(dve, s_rows_out[done.parity], 16 * (done.half + 1))
                    dve.tensor_copy(rows[:, done.parity, :, :], tr[:, :, :])
                    wait(dve, A.score, done.value + 1)
                    dve.tensor_copy(score[:, bass.ds(done.value * RPT, RPT), :].rearrange("p r e -> p (r e)"),
                                    misc[:, 0:RPT * EXP]).then_inc(A.rows, 1)
                if st.within(CHUNKS):
                    dve_hidden(dve, A, st, 0)
                    if (st + 1).within(CHUNKS):
                        split_x(st + 1)
                    wait(dve, s_chi, st.value + 1)
                    dve.tensor_tensor(cexp[:, st.parity, 1, :, :, :],
                                      cexp_raw[:, st.parity, :, :, :].rearrange("p r f c -> p f r c"),
                                      cexp[:, st.parity, 0, :, :, :].bitcast(F32), ALU.subtract)\
                       .then_inc(s_clo, 1)
                    dve_hidden(dve, A, st, 1)
                if (st - 1).within(CHUNKS):
                    c = (st - 1).value
                    wait(dve, A.down, c + 1)
                    wait(dve, A.score, c)
                    dve.tensor_scalar(yT[0:SHARED, :], dn[0:SHARED, :], fc2_bias[:, 0:1], None, ALU.add)
                    for r in range(RPT):
                        ins = dve.tensor_scalar(yT[SHARED:P, r * P:(r + 1) * P],
                                                dx[r * PART:(r + 1) * PART, r * P:(r + 1) * P],
                                                seq_bias[SHARED:P, bass.ds(c * RPT + r, 1)], None, ALU.add)
                    ins.then_inc(A.flat, 1)

            run_steps(dve, CHUNKS, step_a)

            rank_b = rank[:, :].unsqueeze(1).to_broadcast((P, SEQS, EXP))
            dve.wait_ge(A.rows, CHUNKS)
            left = score
            for k in range(TOPK):
                link(dve.tensor_reduce(top[:, k, :], left[:, :, :], AX, ALU.max))
                link(dve.tensor_tensor(same[:, :, :], left[:, :, :],
                                       top[:, k, :].unsqueeze(2).to_broadcast((P, SEQS, EXP)), ALU.is_equal))
                link(dve.tensor_tensor(same_r[:, :, :], same[:, :, :], rank_b, ALU.mult))
                link(dve.tensor_reduce(first[:, k, :], same_r[:, :, :], AX, ALU.max))
                link(dve.tensor_tensor(chosen[:, :, k, :], rank_b,
                                       first[:, k, :].unsqueeze(2).to_broadcast((P, SEQS, EXP)), ALU.is_equal))
                if k == 0:
                    link(dve.scalar_tensor_tensor(rest[:, :, :], chosen[:, :, 0, :], NEG, score[:, :, :],
                                                  ALU.mult, ALU.add))
                    left = rest
            dve.sem_inc(s_chosen, 1)
            dve.tensor_tensor(gap[:, :], top[:, 1, :], top[:, 0, :], ALU.subtract).then_inc(s_gap, 1)

            dve.wait_ge(s_rank, 2)
            link(dve.tensor_copy(total[:, :, :], hp[:, 1, 0:PAIRS * EXP].rearrange("p (j e) -> p e j", e=EXP)))
            link(dve.tensor_tensor_scan(upto[:, :, :].rearrange("p e j -> p (e j)"), ones_f[:, :],
                                        total[:, :, :].rearrange("p e j -> p (e j)"), 0.0, ALU.mult, ALU.add))
            link(dve.tensor_tensor(start[:, :, :], upto[:, :, :], total[:, :, :], ALU.subtract))
            link(dve.tensor_tensor(count[:, :], upto[:, :, PAIRS - 1], start[:, :, 0], ALU.subtract))
            link(dve.tensor_tensor(over[:, :, :], count[:, :].unsqueeze(2).to_broadcast((P, EXP, MAXT)),
                                   fill[:, :].unsqueeze(1).to_broadcast((P, EXP, MAXT)), ALU.is_gt))
            link(dve.tensor_reduce(tiles[:, :], over[:, :, :], AX, ALU.add))
            link(dve.tensor_tensor_scan(tiles_upto[:, :], ones_f[:, 0:EXP], tiles[:, :], 0.0, ALU.mult, ALU.add))
            link(dve.tensor_tensor(tiles_from[:, :], tiles_upto[:, :], tiles[:, :], ALU.subtract))
            link(dve.tensor_tensor(passed[:, :, :], tile_f[:, :].unsqueeze(2).to_broadcast((P, TILES, EXP)),
                                   tiles_upto[:, :].unsqueeze(1).to_broadcast((P, TILES, EXP)), ALU.is_ge))
            link(dve.tensor_reduce(owner_f[:, :], passed[:, :, :], AX, ALU.add))
            dve.tensor_scalar(owner_i[:, :], owner_f[:, :], float(EXP - 1), None, ALU.min).then_inc(s_owner, 1)
            link(dve.scalar_tensor_tensor(shift[:, :], tiles_from[:, :], float(TILE), start[:, :, 0],
                                          ALU.mult, ALU.subtract))
            link(dve.tensor_tensor(place[:, :, :], start[:, :, :].rearrange("p e j -> p j e"),
                                   shift[:, :].unsqueeze(1).to_broadcast((P, PAIRS, EXP)), ALU.add))
            link(dve.tensor_tensor(place_m[:, :, :], place[:, :, :],
                                   hp[:, 0, 0:PAIRS * EXP].rearrange("p (j e) -> p j e", e=EXP), ALU.add))
            link(dve.tensor_tensor(place[:, :, :], place_m[:, :, :],
                                   chosen[:, :, :, :].rearrange("p s k e -> p (s k) e"), ALU.mult))
            link(dve.tensor_reduce(slot[:, :], place[:, :, :], AX, ALU.add))
            link(dve.tensor_copy(slot_i[:, :], slot[:, :]))
            dve.sem_inc(s_slot, 1)
            dve.tensor_scalar(block_i[:, :], slot_i[:, :], 7, None, ALU.logical_shift_right)
            link(dve.tensor_scalar(line_i[:, :], slot_i[:, :], P - 1, None, ALU.bitwise_and))
            dve.tensor_copy(block[:, :], block_i[:, :])
            link(dve.tensor_copy(line[:, :], line_i[:, :]))

            tok_j = tok[:, :, :].rearrange("p s k -> p (s k)")

            def list_half(st):
                n, u = st.value, st.parity
                wait(dve, s_listed, n - 1)
                for i in range(LIST_GROUP):
                    j = bass.ds(n * LIST_GROUP + i, 1)
                    dve.tensor_scalar(line_hot[:, u, i, :], lane[:, :], line[:, j], None, ALU.is_equal)
                    ins = dve.tensor_scalar(block_tok[:, u, i, :], lane[:, 0:BLOCKS], block[:, j],
                                            tok_j[:, j], ALU.is_equal, ALU.mult)
                ins.then_inc(s_line, 1)

            run_pairs(dve, PAIRS // LIST_GROUP, list_half)
            dve.wait_ge(s_listed, PAIRS // LIST_GROUP)
            dve.tensor_scalar(source[:, :], misc[:, 0:BLOCKS], float(TOKEN_SHIFT), None, ALU.add)\
               .then_inc(s_source, 1)

            dve.wait_ge(s_exp, 1)
            link(dve.tensor_scalar(denom[:, :], egap[:, :], 1.0, None, ALU.add))
            link(dve.reciprocal(gate[:, 0, :], denom[:, :]))
            link(dve.tensor_tensor(gate[:, 1, :], egap[:, :], gate[:, 0, :], ALU.mult))

            def split_picked(st):
                wait(dve, C.xhi, st.value + 1)
                dve.tensor_tensor(xs[:, st.parity, 1, :], dx[:, :],
                                  xs[:, st.parity, 0, :].bitcast(F32), ALU.subtract).then_inc(C.xlo, 1)

            def step_c(st):
                if (st - 2).within(TILES):
                    done = st - 2
                    wait(dve, C.turned, done.value + 1)
                    wait(dve, s_zout[done.parity], 16 * (done.half + 1))
                    dve.tensor_copy(rows[:, done.parity, :, :], tr[:, :, :]).then_inc(C.rows, 1)
                if st.within(TILES):
                    dve_hidden(dve, C, st, 0)
                    if (st + 1).within(TILES):
                        split_picked(st + 1)
                    dve_hidden(dve, C, st, 1)
                if (st - 1).within(TILES):
                    wait(dve, C.down, st.value)
                    wait(dve, C.turned, st.value - 1)
                    dve.tensor_copy(yT[:, :], dn[:, :]).then_inc(C.flat, 1)

            split_picked(Step(0, 0))
            run_steps(dve, TILES, step_c)

            dve.wait_ge(s_xrows, 16)
            for u in range(2):
                dve.wait_ge(s_zout[u], 16 * (1 + (TILES + 1 - u) // 2))

            def finish(st):
                t, u = st.value, st.parity
                wait(dve, s_back[u], 16 * FIN_GROUP * TOPK * (st.half + 1))
                wait(dve, s_out[u], 16 * st.half)
                for r in range(FIN_GROUP):
                    z0 = hid[:, u, (2 * r) * P:(2 * r + 1) * P]
                    s = bass.ds(t * FIN_GROUP + r, 1)
                    ins = dve.scalar_tensor_tensor(yT[:, r * P:(r + 1) * P], z0,
                                                   gate[:, 0, s], x_rows[:, s, :].rearrange("p s d -> p (s d)"),
                                                   ALU.mult, ALU.add)
                ins.then_inc(s_half, 1)
                wait(dve, s_half, t + 1)
                for r in range(FIN_GROUP):
                    z1 = hid[:, u, (2 * r + 1) * P:(2 * r + 2) * P]
                    s = bass.ds(t * FIN_GROUP + r, 1)
                    ins = dve.scalar_tensor_tensor(rows[:, u, r, :], z1,
                                                   gate[:, 1, s], yT[:, r * P:(r + 1) * P],
                                                   ALU.mult, ALU.add)
                ins.then_inc(s_fin, 1)
                wait(dve, s_fin, t + 1)

            run_pairs(dve, SEQS // FIN_GROUP, finish)

        @block_ctx.tensor
        def _(pe):
            def step_a(st):
                if st.within(CHUNKS):
                    wait(pe, A.xlo, st.value + 1)
                    pe_up(pe, A, st, 0, fc1)
                if (st - 2).within(CHUNKS):
                    c = (st - 2).value
                    wait(pe, A.flat, c + 1)
                    for r in range(RPT):
                        mm = pe.transpose(tr[:, r, :], yT[:, r * P:(r + 1) * P], ident[:, :])
                    mm.then_inc(A.turned, 1)
                    for r in range(RPT):
                        mm = pe.matmul(misc[:, r * EXP:(r + 1) * EXP], yT[:, r * P:(r + 1) * P],
                                       router[:, :], start=True, stop=True)
                    mm.then_inc(A.score, 1)
                prev = st - 1

                def down(g, last):
                    if prev.within(CHUNKS):
                        u = prev.parity
                        pe_down(pe, A, prev, g,
                                [(dn[0:SHARED, :], lambda w, f: fc2[:, w, f, :]),
                                 (dx[:, :], lambda w, f: cexp[:, u, w, f, :, :].rearrange("p r c -> p (r c)"))],
                                last)

                if prev.within(CHUNKS):
                    wait(pe, s_clo, st.value)
                    wait(pe, A.flat, st.value - 1)
                down(0, False)
                if st.within(CHUNKS):
                    pe_up(pe, A, st, 1, fc1)
                down(1, True)

            pe.wait_ge(s_load[6], 16)
            pe.wait_ge(s_hot, 1)
            pe.matmul(misc[SHARED:P, 0:SEQS], cexp_bias[:, :], seq_hot[:, :], start=True, stop=True)\
              .then_inc(s_bias, 1)
            pe.wait_ge(s_biasc, 1)
            pe.wait_ge(s_fc_lo, 2)
            pe.wait_ge(s_load[7], 16)
            pe.wait_ge(s_const, 12)
            run_steps(pe, CHUNKS, step_a)

            pe.wait_ge(s_chosen, 1)
            pairs_e = chosen[:, :, :, :].rearrange("p s k e -> p (s k e)")
            pe.matmul(hp[:, 0, 0:PAIRS * EXP], before[:, :], pairs_e, start=True, stop=True).then_inc(s_rank, 1)
            pe.matmul(hp[:, 1, 0:PAIRS * EXP], ones_b[:, :], pairs_e, start=True, stop=True).then_inc(s_rank, 1)

            def list_half(n, u, head=False, tail=False):
                wait(pe, s_line, n + 1)
                for i in range(LIST_GROUP):
                    mm = pe.matmul(misc[:, 0:BLOCKS], line_hot[:, u, i, :], block_tok[:, u, i, :],
                                   start=head and i == 0, stop=tail and i == LIST_GROUP - 1)
                mm.then_inc(s_listed, 1)

            halves = PAIRS // LIST_GROUP
            list_half(0, 0, head=True)
            list_half(1, 1)
            with pe.Fori(1, halves // 2 - 1) as i:
                list_half(2 * i, 0)
                list_half(2 * i + 1, 1)
            list_half(halves - 2, 0)
            list_half(halves - 1, 1, tail=True)

            def transpose_picked(st):
                u = st.parity
                wait(pe, s_pick[u], 16 * RPT * (st.half + 1))
                wait(pe, C.xlo, st.value)
                for r in range(RPT):
                    mm = pe.transpose(dx[:, r * P:(r + 1) * P], picked[:, u, r, :], ident[:, :])
                mm.then_inc(C.tin, 1)

            def step_c(st):
                if st.within(TILES):
                    wait(pe, C.xlo, st.value + 1)
                    wait(pe, s_w1[st.parity], 16 * (st.half + 1))
                    pe_up(pe, C, st, 0, w1[:, st.parity, :, :])
                if (st - 2).within(TILES):
                    c = (st - 2).value
                    wait(pe, C.flat, c + 1)
                    for r in range(RPT):
                        mm = pe.transpose(tr[:, r, :], yT[:, r * P:(r + 1) * P], ident[:, :])
                    mm.then_inc(C.turned, 1)
                if (st + 1).within(TILES):
                    transpose_picked(st + 1)
                prev = st - 1

                def down(g, last):
                    if prev.within(TILES):
                        u = prev.parity
                        pe_down(pe, C, prev, g, [(dn[:, :], lambda w, f: w2[:, u, w, f * P:(f + 1) * P])], last)

                if prev.within(TILES):
                    wait(pe, s_w2[prev.parity], 16 * (prev.half + 1))
                    wait(pe, C.flat, st.value - 1)
                down(0, False)
                if st.within(TILES):
                    pe_up(pe, C, st, 1, w1[:, st.parity, :, :])
                down(1, True)

            transpose_picked(Step(0, 0))
            run_steps(pe, TILES, step_c)


def kernel(x, itok_B_0_15, L0_cond_fc1_w, L0_cond_fc1_b, L0_cond_fc2_w, L0_cond_fc2_b,
           L0_cond_experts_w, L0_cond_experts_b, L0_ffn_router_w, L0_ffn_expert_w1, L0_ffn_expert_w2):
    import numpy as np
    import concourse.bacc as bacc
    from concourse.bass_utils import run_bass_kernel_spmd

    x = np.ascontiguousarray(x)
    arrays = {
        "xT": x.reshape(TOKENS, P).T,
        "x": x,
        "itok": np.asarray(itok_B_0_15).reshape(1, SEQS),
        "fc1T": np.asarray(L0_cond_fc1_w).T,
        "fc1_b": np.asarray(L0_cond_fc1_b).reshape(FB, P).T,
        "fc2T": np.asarray(L0_cond_fc2_w).reshape(SHARED, FB, P).transpose(2, 1, 0),
        "fc2_b": np.asarray(L0_cond_fc2_b).reshape(SHARED, 1),
        "cexpT": np.asarray(L0_cond_experts_w).reshape(CEXP, PART, FB, P).transpose(0, 3, 2, 1)
                   .reshape(CEXP, P, FB * PART),
        "cexp_b": np.asarray(L0_cond_experts_b),
        "routerT": np.asarray(L0_ffn_router_w).T,
        "w1T": np.asarray(L0_ffn_expert_w1).transpose(2, 0, 1),
        "w2T": np.asarray(L0_ffn_expert_w2).reshape(EXP, P, FB, P).transpose(3, 0, 2, 1).reshape(P, EXP, HID),
    }
    arrays = {"in_" + k: np.ascontiguousarray(v) for k, v in arrays.items()}
    nc = bacc.Bacc("TRN2", target_bir_lowering=False, num_devices=1)
    args = [nc.dram_tensor(k, v.shape, mybir.dt.from_np(v.dtype), kind="ExternalInput").ap()
            for k, v in arrays.items()]
    out = nc.dram_tensor("out", (SEQS, P, P), F32, kind="ExternalOutput").ap()
    build(nc, *args, out)
    r = run_bass_kernel_spmd(nc, [arrays], core_ids=[0])
    return r.results[0]["out"]
```

```python
from contextlib import ExitStack

import concourse.bass as bass
from concourse import mybir

F32 = mybir.dt.float32
F32R = mybir.dt.float32r
BF16 = mybir.dt.bfloat16
I32 = mybir.dt.int32
ALU = mybir.AluOpType
ACT = mybir.ActivationFunctionType
AX = mybir.AxisListType.X

P = 128
SEQS = 32
TOKENS = SEQS * P
HID = 512
FB = HID // P
GB = FB // 2
PART = 32
SHARED = P - PART
CEXP = 16
EXP = 8
TOPK = 2
TILE = 512
RPT = TILE // P
CHUNKS = TOKENS // TILE
TILES = (TOPK * TOKENS + EXP * (TILE - 1)) // TILE
ROOM = TOKENS // TILE + 1
FILL_TILE = EXP * ROOM
ROW = P + 4
NO_ROW = 1 << 24
POOL_EXP = EXP // 2
LAG = 2
MAXT = 8
FIN_GROUP = 4
GROUPS = SEQS // FIN_GROUP
RING = 4
MISC_RANK, MISC_TOTAL = 64, 96


class Step:

    def __init__(self, pair, offset):
        self.pair, self.offset = pair, offset
        self.value = 2 * pair + offset
        self.parity = offset % 2
        self.half = pair + offset // 2

    def __add__(self, d):
        return Step(self.pair, self.offset + d)

    def __sub__(self, d):
        return self + (-d)

    def within(self, n):
        return not isinstance(self.value, int) or 0 <= self.value < n


def wait(eng, sem, value):
    if not isinstance(value, int) or value > 0:
        eng.wait_ge(sem, value)


def run_steps(eng, n, body, ahead=1):
    pairs = (n - ahead - LAG) // 2
    for s in range(LAG):
        body(Step(0, s))
    with eng.Fori(1, 1 + pairs) as i:
        body(Step(i, 0))
        body(Step(i, 1))
    for s in range(LAG + 2 * pairs, n + LAG):
        body(Step(s // 2, s % 2))


def run_pairs(eng, n, body):
    body(Step(0, 0))
    body(Step(0, 1))
    with eng.Fori(1, n // 2) as i:
        body(Step(i, 0))
        body(Step(i, 1))
    if n % 2:
        body(Step(n // 2, 0))


def build(nc, xT, x, itok, fc1T, fc1_b, fc2T, fc2_b, cexpT, cexp_b, routerT, w1T, w2T, out):
    assert LAG == 2
    slots = nc.dram_tensor("slots", ((FILL_TILE + 1) * TILE, ROW), F32, kind="Internal").ap()
    results = nc.dram_tensor("results", (TOPK * TOKENS, P), F32, kind="Internal").ap()
    slot_tiles = slots.rearrange("(t r p) w -> p t r w", r=RPT, p=P)
    result_seqs = results.rearrange("(k s p) d -> p k s d", k=TOPK, p=P)
    x_all = x.rearrange("s p d -> p s d")
    out_store = out.rearrange("s p d -> p s d")

    with ExitStack() as ctx:
        def sb(name, shape, dt=F32):
            return ctx.enter_context(nc.sbuf_tensor(name, shape, dt))

        def ps(name, shape):
            return ctx.enter_context(nc.psum_tensor(name, shape, F32))

        def sem(name):
            return ctx.enter_context(nc.semaphore(name))

        fc1_raw = sb("fc1_raw", [P, HID])
        fc1 = sb("fc1", [P, 2, HID], F32R)
        fc2_raw = sb("fc2_raw", [P, FB, SHARED])
        fc2 = sb("fc2", [P, 2, FB, SHARED], F32R)
        cexp_raw = sb("cexp_raw", [P, 2, RPT, FB, PART])
        cexp = sb("cexp", [P, 2, 2, FB, RPT, PART], F32R)
        ffn_raw = sb("ffn_raw", [P, 2 * HID])
        ffn = sb("ffn", [P, EXP, 2, 2, HID], F32R)
        z_rows = ffn[:, :, :, :, :].rearrange("p e w h n -> p (e w h n)").bitcast(F32)[:, 0:GROUPS * TOPK * TILE]\
            .rearrange("p (g k n) -> p g k n", g=GROUPS, k=TOPK)
        w1 = sb("w1", [P, 2, 2, HID], F32R)
        w2 = sb("w2", [P, 2, 2, HID], F32R)
        router = sb("router", [P, EXP])
        fc1_bias = sb("fc1_bias", [P, FB])
        fc2_bias = sb("fc2_bias", [SHARED, 1])
        cexp_bias = sb("cexp_bias", [CEXP, PART])
        seq_bias = sb("seq_bias", [P, SEQS])
        x_raw = sb("x_raw", [P, 2, TILE])
        xs = sb("xs", [P, 2, 2, TILE], F32R)
        hid = sb("hid", [P, 2, GB * TILE])
        hs = sb("hs", [P, 2, 2, 2, GB * TILE], F32R)
        yT = sb("yT", [P, TILE])
        y_rows = sb("y_rows", [P, 2, TOPK, RPT, ROW])
        rows = sb("rows", [P, 2, RPT, P])
        picked = sb("picked", [P, 2, RPT, ROW])
        filler = sb("filler", [P, RPT, ROW])
        x_rows = sb("x_rows", [P, SEQS, P])
        pool_raw = x_rows[:, :, :].rearrange("p s d -> p (s d)").rearrange("p (e w n) -> p e w n", e=POOL_EXP, w=2)
        ident = sb("ident", [P, P])
        ones_b = sb("ones_b", [P, P], BF16)
        before = sb("before", [P, P], BF16)
        part_i = sb("part_i", [CEXP, 1], I32)
        part_f = sb("part_f", [CEXP, 1])
        exp_i = sb("exp_i", [P, EXP], I32)
        exp_f = sb("exp_f", [P, EXP])
        room_i = sb("room_i", [P, EXP], I32)
        room = sb("room", [P, EXP])
        fill_i = sb("fill_i", [P, MAXT], I32)
        fill = sb("fill", [P, MAXT])
        tile_i = sb("tile_i", [P, TILES], I32)
        tile_f = sb("tile_f", [P, TILES])
        carry_i = sb("carry_i", [P, EXP, RPT + 1], I32)
        carry = sb("carry", [P, EXP, RPT + 1])
        result_row = sb("result_row", [P, CHUNKS, TOPK, RPT], I32)
        ones_f = sb("ones_f", [P, EXP])
        warm = sb("warm", [P, 1])
        itok_row = sb("itok_row", [1, SEQS], I32)
        itok_all = sb("itok_all", [CEXP, SEQS], I32)
        itok_f = sb("itok_f", [CEXP, SEQS])
        seq_hot = sb("seq_hot", [CEXP, SEQS])
        top = sb("top", [P, RPT, EXP])
        top_exp = sb("top_exp", [P, RPT, EXP], mybir.dt.uint32)
        chosen = sb("chosen", [P, RPT, TOPK, EXP], BF16)
        either = sb("either", [P, RPT, EXP], BF16)
        run = sb("run", [P, EXP, RPT + 1])
        base = sb("base", [P, EXP, RPT + 1])
        place = sb("place", [P, RPT, EXP])
        place_c = sb("place_c", [P, RPT, TOPK, EXP])
        slot_f = sb("slot_f", [P, RPT * TOPK])
        slot = sb("slot", [P, 2, RPT * TOPK], I32)
        gap = sb("gap", [P, SEQS])
        egap = sb("egap", [P, SEQS])
        denom = sb("denom", [P, SEQS])
        gate = sb("gate", [P, TOPK, SEQS])
        count = sb("count", [P, EXP])
        over = sb("over", [P, EXP, MAXT])
        tiles = sb("tiles", [P, EXP])
        tiles_upto = sb("tiles_upto", [P, EXP])
        unused = sb("unused", [P, EXP])
        passed = sb("passed", [P, TILES, EXP])
        skipped = sb("skipped", [P, TILES, EXP])
        owner_f = sb("owner_f", [P, TILES])
        owner_i = sb("owner_i", [P, TILES], I32)
        where_f = sb("where_f", [P, TILES])
        where_t = sb("where_t", [P, TILES])
        where_i = sb("where_i", [P, TILES], I32)
        end_i = sb("end_i", [P, EXP], I32)
        back = sb("back", [P, TILES, RPT], I32)
        back_now = sb("back_now", [P, 2, RPT], I32)

        hp = ps("hp", [P, 2, GB * TILE])
        dn = ps("dn", [P, TILE])
        dx = ps("dx", [P, TILE])
        tr = ps("tr", [P, RPT, P])
        misc = ps("misc", [P, TILE])

        s_const = sem("s_const")
        s_constf = sem("s_constf")
        s_load = [sem(f"s_load{n}") for n in range(9)]
        s_xrows = sem("s_xrows")
        s_xin = [sem(f"s_xin{n}") for n in range(2)]
        s_cexp = [sem(f"s_cexp{n}") for n in range(2)]
        s_pool_w = [sem(f"s_pool_w{n}") for n in range(2)]
        s_pool_hi, s_pool_lo = sem("s_pool_hi"), sem("s_pool_lo")
        s_ffn, s_ffn_hi, s_ffn_lo = sem("s_ffn"), sem("s_ffn_hi"), sem("s_ffn_lo")
        s_fc_hi, s_fc_lo = sem("s_fc_hi"), sem("s_fc_lo")
        s_hot, s_bias, s_biasc = sem("s_hot"), sem("s_bias"), sem("s_biasc")
        s_chi, s_clo = sem("s_chi"), sem("s_clo")
        s_chain = sem("s_chain")
        s_route = sem("s_route")
        s_either, s_ranked = sem("s_either"), sem("s_ranked")
        s_slot = sem("s_slot")
        s_spread = [sem(f"s_spread{n}") for n in range(2)]
        s_yfree, s_zfree = sem("s_yfree"), sem("s_zfree")
        s_gap, s_exp = sem("s_gap"), sem("s_exp")
        s_end, s_where = sem("s_end"), sem("s_where")
        s_filler, s_fillout = sem("s_filler"), sem("s_fillout")
        s_go, s_sp_go, s_dve_go = sem("s_go"), sem("s_sp_go"), sem("s_dve_go")
        s_pick = [sem(f"s_pick{n}") for n in range(2)]
        s_w1 = [sem(f"s_w1{n}") for n in range(2)]
        s_w2 = [sem(f"s_w2{n}") for n in range(2)]
        s_back = sem("s_back")
        s_zout = [sem(f"s_zout{n}") for n in range(2)]
        s_z = [sem(f"s_z{n}") for n in range(RING)]
        s_half, s_fin = sem("s_half"), sem("s_fin")
        s_out = sem("s_out")

        class Counts:

            def __init__(self, tag, per_group):
                self.per = per_group
                self.xhi = sem(tag + "xhi")
                self.xlo = sem(tag + "xlo")
                self.up = sem(tag + "up")
                self.gelu = sem(tag + "gelu")
                self.hi = sem(tag + "hi")
                self.lo = sem(tag + "lo")
                self.down = sem(tag + "down")
                self.flat = sem(tag + "flat")
                self.flat2 = sem(tag + "flat2")
                self.turned = sem(tag + "turned")
                self.rows = sem(tag + "rows")
                self.rows2 = sem(tag + "rows2")
                self.tin = sem(tag + "tin")
                self.score = sem(tag + "score")

        A, C = Counts("a_", GB), Counts("c_", 1)

        def pe_up(pe, k, st, g, weight):
            wait(pe, k.gelu, 2 * k.per * (st.value - 1) + k.per * (g + 1))
            for n in range(GB):
                cols = slice((g * GB + n) * P, (g * GB + n + 1) * P)
                dst = hp[:, g, n * TILE:(n + 1) * TILE]
                passes = [(0, 1), (1, 0), (0, 0)]
                for m, (w, v) in enumerate(passes):
                    mm = pe.matmul(dst, weight[:, w, cols], xs[:, st.parity, v, :],
                                   start=m == 0, stop=m == len(passes) - 1)
                if k.per == GB or n == GB - 1:
                    mm.then_inc(k.up, 1)

        def pe_down(pe, k, st, g, products, last_inc):
            wait(pe, k.lo, 2 * st.value + g + 1)
            for dst, weight in products:
                for n in range(GB):
                    f = g * GB + n
                    for m, (w, v) in enumerate([(0, 1), (1, 0), (0, 0)]):
                        mm = pe.matmul(dst, weight(w, f), hs[:, st.parity, v, g, n * TILE:(n + 1) * TILE],
                                       start=(f == 0 and m == 0), stop=(f == FB - 1 and m == 2))
            if last_inc:
                mm.then_inc(k.down, 1)

        def act_hidden(act, k, st, g, bias):
            wait(act, k.lo, 2 * (st.value - 1) + g + 1)
            n_per = GB // k.per
            for n in range(k.per):
                wait(act, k.up, 2 * k.per * st.value + k.per * g + n + 1)
                cols = slice(n * n_per * TILE, (n + 1) * n_per * TILE)
                if bias is None:
                    ins = act.activation(hid[:, g, cols], hp[:, g, cols], ACT.Gelu)
                else:
                    f = g * GB + n
                    ins = act.activation(hid[:, g, cols], hp[:, g, cols], ACT.Gelu, bias=bias[:, f:f + 1])
                ins.then_inc(k.gelu, 1)
            wait(act, k.gelu, 2 * k.per * st.value + k.per * (g + 1))
            wait(act, k.down, st.value - 1)
            act.activation(hs[:, st.parity, 0, g, :], hid[:, g, :], ACT.Copy).then_inc(k.hi, 1)

        def dve_hidden(dve, k, st, g):
            wait(dve, k.hi, 2 * st.value + g + 1)
            dve.tensor_tensor(hs[:, st.parity, 1, g, :], hid[:, g, :],
                              hs[:, st.parity, 0, g, :].bitcast(F32), ALU.subtract).then_inc(k.lo, 1)

        block_ctx = ctx.enter_context(nc.Block())

        @block_ctx.sync
        def _(sp):
            sp.dma_start(itok_row[:, :], itok).then_inc(s_load[0], 16)
            sp.dma_start(x_raw[:, 0, :], xT[:, 0:TILE]).then_inc(s_xin[0], 16)
            sp.dma_start(fc1_raw[:, :], fc1T).then_inc(s_load[1], 16)
            sp.dma_start(fc1_bias[:, :], fc1_b).then_inc(s_load[2], 16)
            sp.dma_start(fc2_raw[:, :, :], fc2T).then_inc(s_load[3], 16)
            sp.dma_start(fc2_bias[:, :], fc2_b).then_inc(s_load[4], 16)
            sp.dma_start(itok_all[:, :], itok.to_broadcast((CEXP, SEQS))).then_inc(s_load[5], 16)
            sp.dma_start(cexp_bias[:, :], cexp_b).then_inc(s_load[6], 16)
            sp.dma_start(router[:, :], routerT).then_inc(s_load[7], 16)

            def is_first(st):
                return isinstance(st.value, int) and st.value == 0

            def load_chunk(st):
                c, u = st.value, st.parity
                if not isinstance(c, int) or c > 0:
                    wait(sp, A.xlo, c - 1)
                    sp.dma_start(x_raw[:, u, :], xT[:, bass.ds(c * TILE, TILE)]).then_inc(s_xin[u], 16)
                wait(sp, s_clo, c - 1)
                sp.wait_ge(s_load[0], 16)
                sp.sem_inc(s_sp_go, 1)
                for r in range(RPT):
                    e = sp.value_load(itok_row[0:1, bass.ds(c * RPT + r, 1)], min_val=0, max_val=CEXP - 1)
                    sp.dma_start(cexp_raw[:, u, r, :, :].rearrange("p f c -> p (f c)"),
                                 cexpT[bass.ds(e, 1), :, :].rearrange("e p n -> p (e n)"))\
                      .then_inc(s_cexp[u], 16)

            def step_a(st):
                if (st + 1).within(CHUNKS) and not is_first(st):
                    load_chunk(st + 1)
                if st.parity == 0 and (st + 1).within(CHUNKS):
                    e = POOL_EXP + st.half
                    wait(sp, s_ffn_lo, st.half)
                    for n, w in enumerate((w1T, w2T)):
                        sp.dma_start(ffn_raw[:, n * HID:(n + 1) * HID],
                                     w[:, bass.ds(e, 1), :].rearrange("p e n -> p (e n)")).then_inc(s_ffn, 16)

            load_chunk(Step(0, 0))
            load_chunk(Step(0, 1))
            for h in range(2):
                for n, w in enumerate((w1T, w2T)):
                    half = slice(h * POOL_EXP // 2, (h + 1) * POOL_EXP // 2)
                    sp.dma_start(pool_raw[:, half, n, :], w[:, half, :]).then_inc(s_pool_w[h], 16)
            sp.wait_ge(s_filler, 2)
            sp.dma_start(slot_tiles[:, FILL_TILE, :, :], filler[:, :, :]).then_inc(s_fillout, 16)
            run_steps(sp, CHUNKS, step_a)
            sp.wait_ge(s_pool_lo, POOL_EXP)
            sp.dma_start(x_rows[:, :, :], x_all).then_inc(s_xrows, 16)

            def load_weights(st, which, dst, sems):
                sp.sem_inc(s_sp_go, 1)
                e = sp.value_load(owner_i[0:1, bass.ds(st.value, 1)], min_val=0, max_val=EXP - 1)
                sp.dma_start(dst[:, st.parity, :, :].rearrange("p h n -> p (h n)").bitcast(F32),
                             ffn[:, bass.ds(e, 1), which, :, :].rearrange("p e h n -> p (e h n)").bitcast(F32))\
                  .then_inc(sems[st.parity], 16)

            def load_picked(st):
                t = sp.value_load(where_i[0:1, bass.ds(st.value, 1)], min_val=0, max_val=FILL_TILE)
                sp.dma_start(picked[:, st.parity, :, :],
                             slot_tiles[:, bass.ds(t, 1), :, :].rearrange("p t r w -> p (t r) w"))\
                  .then_inc(s_pick[st.parity], 16)

            def step_c(st):
                if (st + 1).within(TILES):
                    wait(sp, C.up, 2 * st.value)
                    load_weights(st + 1, 0, w1, s_w1)
                if (st + 2).within(TILES):
                    wait(sp, C.xlo, st.value + 1)
                    sp.sem_inc(s_sp_go, 1)
                    load_picked(st + 2)
                if st.within(TILES):
                    wait(sp, C.down, st.value - 1)
                    load_weights(st, 1, w2, s_w2)

            sp.wait_ge(s_end, 1)
            for e in range(EXP):
                row = sp.value_load(end_i[0:1, e:e + 1], min_val=e * ROOM * TILE,
                                    max_val=e * ROOM * TILE + TOKENS)
                sp.dma_start(slots[bass.ds(row, TILE), :].rearrange("(r p) w -> p r w", p=P), filler[:, :, :])\
                  .then_inc(s_fillout, 16)
            sp.wait_ge(s_where, 1)
            sp.wait_ge(s_pool_lo, POOL_EXP)
            sp.wait_ge(s_ffn_lo, EXP - POOL_EXP)
            load_weights(Step(0, 0), 0, w1, s_w1)
            sp.wait_ge(s_fillout, 16 * (EXP + 1))
            for u in range(2):
                sp.wait_ge(s_spread[u], 16 * RPT * TOPK * (CHUNKS // 2))
            load_picked(Step(0, 0))
            load_picked(Step(0, 1))
            run_steps(sp, TILES, step_c, ahead=2)

            for u in range(2):
                sp.wait_ge(s_zout[u], 16 * RPT * ((TILES + 1 - u) // 2))

            def load_z(g):
                for k in range(TOPK):
                    sp.dma_start(z_rows[:, g, k, :].rearrange("p (s d) -> p s d", d=P),
                                 result_seqs[:, k, g * FIN_GROUP:(g + 1) * FIN_GROUP, :])\
                      .then_inc(s_z[g % RING], 16)

            for g in range(RING):
                load_z(g)
            for g in range(GROUPS):
                sp.wait_ge(s_fin, g + 1)
                sp.dma_start(out_store[:, g * FIN_GROUP:(g + 1) * FIN_GROUP, :],
                             z_rows[:, g, 0, :].rearrange("p (s d) -> p s d", d=P)).then_inc(s_out, 16)
                if g + RING < GROUPS:
                    load_z(g + RING)
            sp.wait_ge(s_out, 16 * GROUPS)

        @block_ctx.gpsimd
        def _(pool):
            pool.memset(ones_f[:, :], 1.0).then_inc(s_const, 1)
            pool.memset(ident[:, :], 1.0).then_inc(s_const, 1)
            pool.memset(before[:, :], 1.0).then_inc(s_const, 1)
            pool.memset(ones_b[:, :], 1.0).then_inc(s_const, 1)
            pool.memset(filler[:, :, :], 0.0).then_inc(s_filler, 1)
            pool.memset(y_rows[:, :, :, :, P:ROW], 0.0).then_inc(s_const, 1)
            pool.iota(part_i[:, :], [[0, 1]], base=0, channel_multiplier=1).then_inc(s_const, 1)
            pool.iota(exp_i[:, :], [[1, EXP]], base=0, channel_multiplier=0).then_inc(s_const, 1)
            pool.iota(room_i[:, :], [[ROOM * TILE, EXP]], base=0, channel_multiplier=0).then_inc(s_const, 1)
            pool.iota(fill_i[:, :], [[TILE, MAXT]], base=0, channel_multiplier=0).then_inc(s_const, 1)
            pool.iota(tile_i[:, :], [[1, TILES]], base=0, channel_multiplier=0).then_inc(s_const, 1)
            pool.iota(carry_i[:, :, :], [[0, EXP], [1, RPT + 1]], base=0, channel_multiplier=0)\
                .then_inc(s_const, 1)
            pool.iota(result_row[:, :, :, :], [[TILE, CHUNKS], [TOKENS, TOPK], [P, RPT]], base=0,
                      channel_multiplier=1).then_inc(s_const, 1)
            pool.wait_ge(s_const, 12)
            pool.affine_select(out=ident[:, :], in_=ident[:, :], compare_op=ALU.is_equal, fill=0.0,
                               base=0, pattern=[[-1, P]], channel_multiplier=1).then_inc(s_const, 1)
            pool.affine_select(out=before[:, :], in_=before[:, :], compare_op=ALU.is_gt, fill=0.0,
                               base=0, pattern=[[1, P]], channel_multiplier=-1).then_inc(s_const, 1)
            pool.wait_ge(s_filler, 1)
            pool.memset(filler[:, :, P:P + 1].bitcast(I32), NO_ROW).then_inc(s_filler, 1)

            with pool.Fori(0, POOL_EXP) as e:
                hi = ffn[:, bass.ds(e, 1), :, 0, :].rearrange("p e w n -> p (e w) n")
                lo = ffn[:, bass.ds(e, 1), :, 1, :].rearrange("p e w n -> p (e w) n")
                raw = pool_raw[:, bass.ds(e, 1), :, :].rearrange("p e w n -> p (e w) n")
                wait(pool, s_pool_hi, e + 1)
                pool.tensor_tensor(lo, raw, hi.bitcast(F32), ALU.subtract).then_inc(s_pool_lo, 1)

            pool.sem_inc(s_yfree, 2)
            pool.sem_inc(s_zfree, 2)

            def free_rows(before, sems, scatters, free):
                if not isinstance(before.value, int) or before.value >= 0:
                    wait(pool, sems[before.parity], 16 * scatters * (before.half + 1))
                    pool.sem_inc(free, 1)

            def spread(st):
                c, u = st.value, st.parity
                wait(pool, A.rows, c + 1)
                wait(pool, A.rows2, c + 1)
                wait(pool, s_slot, c + 1)
                pool.sem_inc(s_go, 1)
                for r in range(RPT):
                    if r == RPT // 2:
                        free_rows(st - 1, s_spread, RPT * TOPK, s_yfree)
                        pool.sem_inc(s_go, 1)
                    for k in range(TOPK):
                        n = r * TOPK + k
                        pool.indirect_dma_start(
                            out=slots, out_offset=bass.IndirectOffsetOnAxis(ap=slot[:, u, n:n + 1], axis=0),
                            in_=y_rows[:, u, k, r, :], in_offset=None).then_inc(s_spread[u], 16)

            run_pairs(pool, CHUNKS, spread)

            def send_back(st):
                t, u = st.value, st.parity
                wait(pool, C.rows, t + 1)
                pool.tensor_copy(back_now[:, u, :], back[:, bass.ds(t, 1), :].rearrange("p t r -> p (t r)"))\
                    .then_inc(s_back, 1)
                wait(pool, s_back, t + 1)
                pool.sem_inc(s_go, 1)
                for r in range(RPT):
                    if r == RPT // 2:
                        free_rows(st - 1, s_zout, RPT, s_zfree)
                        pool.sem_inc(s_go, 1)
                    pool.indirect_dma_start(
                        out=results, out_offset=bass.IndirectOffsetOnAxis(ap=back_now[:, u, r:r + 1], axis=0),
                        in_=rows[:, u, r, :], in_offset=None,
                        bounds_check=TOPK * TOKENS - 1, oob_is_err=False).then_inc(s_zout[u], 16)

            run_pairs(pool, TILES, send_back)

        @block_ctx.scalar
        def _(act):
            act.wait_ge(s_const, 1)
            act.activation(warm[:, :], ones_f[:, 0:1], ACT.Gelu)
            act.wait_ge(s_load[1], 16)
            act.activation(fc1[:, 0, :], fc1_raw[:, :], ACT.Copy).then_inc(s_fc_hi, 1)

            def split_x(st):
                wait(act, s_xin[st.parity], 16 * st.half + 16)
                act.activation(xs[:, st.parity, 0, :], x_raw[:, st.parity, :], ACT.Copy).then_inc(A.xhi, 1)

            split_x(Step(0, 0))
            act.wait_ge(s_load[3], 16)
            act.activation(fc2[:, 0, :, :], fc2_raw[:, :, :], ACT.Copy).then_inc(s_fc_hi, 1)
            act.wait_ge(s_load[2], 16)

            def staged_high(h):
                wait(act, s_pool_w[h], 32)
                for e in range(h * POOL_EXP // 2, (h + 1) * POOL_EXP // 2):
                    act.activation(ffn[:, e, :, 0, :], pool_raw[:, e, :, :], ACT.Copy).then_inc(s_pool_hi, 1)

            def step_a(st):
                second = isinstance(st.value, int) and st.value == 1
                if st.within(CHUNKS):
                    act_hidden(act, A, st, 0, fc1_bias)
                if (st - 2).within(CHUNKS):
                    done = st - 2
                    wait(act, A.turned, done.value + 1)
                    wait(act, A.rows, done.value + 1)
                    act.activation(y_rows[:, done.parity, 1, :, 0:P], tr[:, :, :], ACT.Copy)\
                       .then_inc(A.rows2, 1)
                if st.within(CHUNKS):
                    if (st + 1).within(CHUNKS):
                        split_x(st + 1)
                    wait(act, s_cexp[st.parity], 16 * RPT * (st.half + 1))
                    act.activation(cexp[:, st.parity, 0, :, :, :],
                                   cexp_raw[:, st.parity, :, :, :].rearrange("p r f c -> p f r c"),
                                   ACT.Copy).then_inc(s_chi, 1)
                    if st.parity == 1:
                        wait(act, s_ffn, 32 * (st.half + 1))
                        act.activation(ffn[:, bass.ds(POOL_EXP + st.half, 1), :, 0, :]
                                       .rearrange("p e w n -> p (e w) n"),
                                       ffn_raw[:, :].rearrange("p (w n) -> p w n", w=2), ACT.Copy)\
                           .then_inc(s_ffn_hi, 1)
                    if second:
                        staged_high(0)
                    act_hidden(act, A, st, 1, fc1_bias)
                if (st - 1).within(CHUNKS):
                    c = (st - 1).value
                    wait(act, A.down, c + 1)
                    wait(act, A.score, c)
                    act.activation(yT[0:SHARED, :], dn[0:SHARED, :], ACT.Identity, bias=fc2_bias[:, 0:1])\
                       .then_inc(A.flat2, 1)
                    if second:
                        staged_high(1)

            act.wait_ge(s_load[4], 16)
            run_steps(act, CHUNKS, step_a)

            act.wait_ge(s_gap, 1)
            act.activation(egap[:, :], gap[:, :], ACT.Exp).then_inc(s_exp, 1)
            act.activation(warm[:, :], ones_f[:, 0:1], ACT.Gelu)

            def split_picked(st):
                wait(act, C.tin, st.value + 1)
                act.activation(xs[:, st.parity, 0, :], dx[:, :], ACT.Copy).then_inc(C.xhi, 1)

            def step_c(st):
                if st.within(TILES):
                    act_hidden(act, C, st, 0, None)
                    if (st + 1).within(TILES):
                        split_picked(st + 1)
                    act_hidden(act, C, st, 1, None)

            split_picked(Step(0, 0))
            run_steps(act, TILES, step_c)

        @block_ctx.vector
        def _(dve):
            links = [0]

            def link(ins):
                links[0] += 1
                ins.then_inc(s_chain, 1)
                dve.wait_ge(s_chain, links[0])

            dve.wait_ge(s_fc_hi, 1)
            dve.tensor_tensor(fc1[:, 1, :], fc1_raw[:, :], fc1[:, 0, :].bitcast(F32), ALU.subtract)\
               .then_inc(s_fc_lo, 1)

            def split_x(st):
                wait(dve, A.xhi, st.value + 1)
                dve.tensor_tensor(xs[:, st.parity, 1, :], x_raw[:, st.parity, :],
                                  xs[:, st.parity, 0, :].bitcast(F32), ALU.subtract).then_inc(A.xlo, 1)

            split_x(Step(0, 0))
            dve.wait_ge(s_const, 14)
            dve.tensor_copy(part_f[:, :], part_i[:, :])
            dve.tensor_copy(exp_f[:, :], exp_i[:, :])
            dve.tensor_copy(room[:, :], room_i[:, :])
            dve.tensor_copy(run[:, :, 0], room_i[:, :])
            dve.tensor_copy(fill[:, :], fill_i[:, :])
            dve.tensor_copy(tile_f[:, :], tile_i[:, :])
            dve.tensor_scalar(carry[:, :, :], carry_i[:, :, :], 1.0, None, ALU.min)
            dve.wait_ge(s_load[5], 16)
            link(dve.tensor_copy(itok_f[:, :], itok_all[:, :]))
            dve.tensor_scalar(seq_hot[:, :], itok_f[:, :], part_f[:, 0:1], None, ALU.is_equal)\
               .then_inc(s_hot, 1)
            dve.wait_ge(s_fc_hi, 2)
            dve.tensor_tensor(fc2[:, 1, :, :], fc2_raw[:, :, :], fc2[:, 0, :, :].bitcast(F32), ALU.subtract)\
               .then_inc(s_fc_lo, 1)
            dve.wait_ge(s_bias, 1)
            dve.tensor_copy(seq_bias[SHARED:P, :], misc[SHARED:P, 0:SEQS]).then_inc(s_biasc, 1)
            dve.wait_ge(s_biasc, 1)

            LINKS = 8

            def linker(c):
                n = [0]

                def link_c(ins):
                    n[0] += 1
                    ins.then_inc(s_route, 1)
                    wait(dve, s_route, LINKS * c + n[0])
                return link_c, n

            def choose(st, link_c):
                dve.sem_inc(s_dve_go, 1)
                for r in range(RPT):
                    ins = dve.max(top[:, r, :], misc[:, r * EXP:(r + 1) * EXP])
                link_c(ins)
                dve.sem_inc(s_dve_go, 1)
                for r in range(RPT):
                    ins = dve.max_index(top_exp[:, r, :], top[:, r, :], misc[:, r * EXP:(r + 1) * EXP])
                link_c(ins)
                seqs = bass.ds(st.value * RPT, RPT)
                dve.tensor_tensor(gap[:, seqs], top[:, :, 1], top[:, :, 0], ALU.subtract)
                link_c(dve.tensor_tensor(
                    chosen[:, :, :, :], exp_f[:, :].unsqueeze(1).unsqueeze(1).to_broadcast((P, RPT, TOPK, EXP)),
                    top_exp[:, :, 0:TOPK].unsqueeze(3).to_broadcast((P, RPT, TOPK, EXP)), ALU.is_equal))
                dve.tensor_tensor(either[:, :, :], chosen[:, :, 0, :], chosen[:, :, 1, :], ALU.add)\
                   .then_inc(s_either, 1)

            def place_pairs(st, link_c):
                wait(dve, s_ranked, st.value + 1)
                link_c(dve.tensor_copy(run[:, :, 1:RPT + 1],
                                       misc[:, MISC_TOTAL:MISC_TOTAL + RPT * EXP]
                                       .rearrange("p (r e) -> p e r", e=EXP)))
                link_c(dve.tensor_tensor_scan(base[:, :, :].rearrange("p e r -> p (e r)"),
                                              carry[:, :, :].rearrange("p e r -> p (e r)"),
                                              run[:, :, :].rearrange("p e r -> p (e r)"), 0.0,
                                              ALU.mult, ALU.add))
                dve.tensor_copy(run[:, :, 0], base[:, :, RPT])
                link_c(dve.tensor_tensor(place[:, :, :], base[:, :, 0:RPT].rearrange("p e r -> p r e"),
                                         misc[:, MISC_RANK:MISC_RANK + RPT * EXP]
                                         .rearrange("p (r e) -> p r e", e=EXP), ALU.add))
                link_c(dve.tensor_tensor(place_c[:, :, :, :],
                                         place[:, :, :].unsqueeze(2).to_broadcast((P, RPT, TOPK, EXP)),
                                         chosen[:, :, :, :], ALU.mult))
                link_c(dve.tensor_reduce(slot_f[:, :], place_c[:, :, :, :].rearrange("p r k e -> p (r k) e"),
                                         AX, ALU.add))
                dve.tensor_copy(slot[:, st.parity, :], slot_f[:, :]).then_inc(s_slot, 1)

            def step_a(st):
                done = st - 2
                link_c, n = linker(done.value)
                if done.within(CHUNKS):
                    wait(dve, A.turned, done.value + 1)
                    wait(dve, s_yfree, done.value + 1)
                    dve.tensor_copy(y_rows[:, done.parity, :, :, P:P + 1].bitcast(I32)
                                    .rearrange("p k r w -> p (k r w)"),
                                    result_row[:, bass.ds(done.value, 1), :, :].rearrange("p c k r -> p (c k r)"))
                    dve.tensor_copy(y_rows[:, done.parity, 0, :, 0:P], tr[:, :, :]).then_inc(A.rows, 1)
                    wait(dve, A.score, done.value + 1)
                    choose(done, link_c)
                if st.within(CHUNKS):
                    dve_hidden(dve, A, st, 0)
                    if (st + 1).within(CHUNKS):
                        split_x(st + 1)
                    wait(dve, s_chi, st.value + 1)
                    dve.tensor_tensor(cexp[:, st.parity, 1, :, :, :],
                                      cexp_raw[:, st.parity, :, :, :].rearrange("p r f c -> p f r c"),
                                      cexp[:, st.parity, 0, :, :, :].bitcast(F32), ALU.subtract)\
                       .then_inc(s_clo, 1)
                    if st.parity == 1:
                        wait(dve, s_ffn_hi, st.half + 1)
                        e = bass.ds(POOL_EXP + st.half, 1)
                        dve.tensor_tensor(ffn[:, e, :, 1, :].rearrange("p e w n -> p (e w) n"),
                                          ffn_raw[:, :].rearrange("p (w n) -> p w n", w=2),
                                          ffn[:, e, :, 0, :].rearrange("p e w n -> p (e w) n").bitcast(F32),
                                          ALU.subtract).then_inc(s_ffn_lo, 1)
                if done.within(CHUNKS):
                    place_pairs(done, link_c)
                    assert n[0] == LINKS
                if (st - 1).within(CHUNKS):
                    c = (st - 1).value
                    wait(dve, A.down, c + 1)
                    wait(dve, A.score, c)
                    for r in range(RPT):
                        ins = dve.tensor_scalar(yT[SHARED:P, r * P:(r + 1) * P],
                                                dx[r * PART:(r + 1) * PART, r * P:(r + 1) * P],
                                                seq_bias[SHARED:P, bass.ds(c * RPT + r, 1)], None, ALU.add)
                    ins.then_inc(A.flat, 1)
                if st.within(CHUNKS):
                    dve_hidden(dve, A, st, 1)

            run_steps(dve, CHUNKS, step_a)

            dve.sem_inc(s_gap, 1)
            link(dve.tensor_copy(end_i[:, :], run[:, :, 0]))
            dve.sem_inc(s_end, 1)
            link(dve.tensor_tensor(count[:, :], run[:, :, 0], room[:, :], ALU.subtract))
            link(dve.tensor_tensor(over[:, :, :], count[:, :].unsqueeze(2).to_broadcast((P, EXP, MAXT)),
                                   fill[:, :].unsqueeze(1).to_broadcast((P, EXP, MAXT)), ALU.is_gt))
            link(dve.tensor_reduce(tiles[:, :], over[:, :, :], AX, ALU.add))
            dve.tensor_scalar(unused[:, :], tiles[:, :], -1.0, float(ROOM), ALU.mult, ALU.add)
            link(dve.tensor_tensor_scan(tiles_upto[:, :], ones_f[:, :], tiles[:, :], 0.0, ALU.mult, ALU.add))
            link(dve.tensor_tensor(passed[:, :, :], tile_f[:, :].unsqueeze(2).to_broadcast((P, TILES, EXP)),
                                   tiles_upto[:, :].unsqueeze(1).to_broadcast((P, TILES, EXP)), ALU.is_ge))
            dve.tensor_reduce(owner_f[:, :], passed[:, :, :], AX, ALU.add)
            link(dve.tensor_tensor(skipped[:, :, :], passed[:, :, :],
                                   unused[:, :].unsqueeze(1).to_broadcast((P, TILES, EXP)), ALU.mult))
            link(dve.tensor_reduce(where_f[:, :], skipped[:, :, :], AX, ALU.add))
            link(dve.tensor_tensor(where_t[:, :], where_f[:, :], tile_f[:, :], ALU.add))
            dve.tensor_scalar(where_i[:, :], where_t[:, :], float(FILL_TILE), None, ALU.min)
            dve.tensor_scalar(owner_i[:, :], owner_f[:, :], float(EXP - 1), None, ALU.min).then_inc(s_where, 1)

            dve.wait_ge(s_exp, 1)
            link(dve.tensor_scalar(denom[:, :], egap[:, :], 1.0, None, ALU.add))
            link(dve.reciprocal(gate[:, 0, :], denom[:, :]))
            link(dve.tensor_tensor(gate[:, 1, :], egap[:, :], gate[:, 0, :], ALU.mult))

            def split_picked(st):
                wait(dve, C.xhi, st.value + 1)
                dve.tensor_copy(back[:, bass.ds(st.value, 1), :].rearrange("p t r -> p (t r)"),
                                picked[:, st.parity, :, P:P + 1].bitcast(I32).rearrange("p r w -> p (r w)"))
                dve.tensor_tensor(xs[:, st.parity, 1, :], dx[:, :],
                                  xs[:, st.parity, 0, :].bitcast(F32), ALU.subtract).then_inc(C.xlo, 1)

            def step_c(st):
                if (st - 2).within(TILES):
                    done = st - 2
                    wait(dve, C.turned, done.value + 1)
                    wait(dve, s_zfree, done.value + 1)
                    dve.tensor_copy(rows[:, done.parity, :, :], tr[:, :, :]).then_inc(C.rows, 1)
                if st.within(TILES):
                    dve_hidden(dve, C, st, 0)
                    if (st + 1).within(TILES):
                        split_picked(st + 1)
                if (st - 1).within(TILES):
                    wait(dve, C.down, st.value)
                    wait(dve, C.turned, st.value - 1)
                    dve.tensor_copy(yT[:, :], dn[:, :]).then_inc(C.flat, 1)
                if st.within(TILES):
                    dve_hidden(dve, C, st, 1)

            split_picked(Step(0, 0))
            run_steps(dve, TILES, step_c)

            dve.wait_ge(s_xrows, 16)

            def finish(i, j):
                g = i * RING + j
                wait(dve, s_z[j], 16 * TOPK * (i + 1))
                z0, z1 = (z_rows[:, bass.ds(g, 1), k, :].rearrange("p g (s d) -> p (g s) d", d=P)
                          for k in range(TOPK))
                for r in range(FIN_GROUP):
                    s = bass.ds(g * FIN_GROUP + r, 1)
                    ins = dve.scalar_tensor_tensor(z0[:, r, :], z0[:, r, :], gate[:, 0, s],
                                                   x_rows[:, s, :].rearrange("p s d -> p (s d)"),
                                                   ALU.mult, ALU.add)
                ins.then_inc(s_half, 1)
                wait(dve, s_half, g + 1)
                for r in range(FIN_GROUP):
                    s = bass.ds(g * FIN_GROUP + r, 1)
                    ins = dve.scalar_tensor_tensor(z0[:, r, :], z1[:, r, :], gate[:, 1, s], z0[:, r, :],
                                                   ALU.mult, ALU.add)
                ins.then_inc(s_fin, 1)

            with dve.Fori(0, GROUPS // RING) as i:
                for j in range(RING):
                    finish(i, j)

        @block_ctx.tensor
        def _(pe):
            def step_a(st):
                if st.within(CHUNKS):
                    wait(pe, A.xlo, st.value + 1)
                    pe_up(pe, A, st, 0, fc1)
                if isinstance(st.value, int) and st.value == 0:
                    setup()
                if (st - 2).within(CHUNKS):
                    c = (st - 2).value
                    wait(pe, A.flat, c + 1)
                    wait(pe, A.flat2, c + 1)
                    wait(pe, A.rows2, c)
                    for r in range(RPT):
                        mm = pe.transpose(tr[:, r, :], yT[:, r * P:(r + 1) * P], ident[:, :])
                    mm.then_inc(A.turned, 1)
                    for r in range(RPT):
                        mm = pe.matmul(misc[:, r * EXP:(r + 1) * EXP], yT[:, r * P:(r + 1) * P],
                                       router[:, :], start=True, stop=True)
                    mm.then_inc(A.score, 1)
                prev = st - 1

                def down(g, last):
                    if prev.within(CHUNKS):
                        u = prev.parity
                        pe_down(pe, A, prev, g,
                                [(dn[0:SHARED, :], lambda w, f: fc2[:, w, f, :]),
                                 (dx[:, :], lambda w, f: cexp[:, u, w, f, :, :].rearrange("p r c -> p (r c)"))],
                                last)

                if prev.within(CHUNKS):
                    wait(pe, s_clo, st.value)
                    wait(pe, A.flat, st.value - 1)
                    wait(pe, A.flat2, st.value - 1)
                down(0, False)
                if st.within(CHUNKS):
                    pe_up(pe, A, st, 1, fc1)
                if (st - 2).within(CHUNKS):
                    wait(pe, s_either, st.value - 1)
                    pairs = either[:, :, :].rearrange("p r e -> p (r e)")
                    pe.matmul(misc[:, MISC_RANK:MISC_RANK + RPT * EXP], before[:, :], pairs,
                              start=True, stop=True)
                    pe.matmul(misc[:, MISC_TOTAL:MISC_TOTAL + RPT * EXP], ones_b[:, :], pairs,
                              start=True, stop=True).then_inc(s_ranked, 1)
                down(1, True)

            def setup():
                pe.wait_ge(s_load[6], 16)
                pe.wait_ge(s_hot, 1)
                pe.matmul(misc[SHARED:P, 0:SEQS], cexp_bias[:, :], seq_hot[:, :], start=True, stop=True)\
                  .then_inc(s_bias, 1)
                pe.wait_ge(s_load[7], 16)
                pe.wait_ge(s_const, 14)
                pe.wait_ge(s_fc_lo, 2)
                pe.wait_ge(s_biasc, 1)

            pe.wait_ge(s_fc_lo, 1)
            run_steps(pe, CHUNKS, step_a)

            def transpose_picked(st):
                u = st.parity
                wait(pe, s_pick[u], 16 * (st.half + 1))
                wait(pe, C.xlo, st.value)
                for r in range(RPT):
                    mm = pe.transpose(dx[:, r * P:(r + 1) * P], picked[:, u, r, 0:P], ident[:, :])
                mm.then_inc(C.tin, 1)

            def step_c(st):
                if st.within(TILES):
                    wait(pe, C.xlo, st.value + 1)
                    wait(pe, s_w1[st.parity], 16 * (st.half + 1))
                    pe_up(pe, C, st, 0, w1[:, st.parity, :, :])
                if (st - 2).within(TILES):
                    c = (st - 2).value
                    wait(pe, C.flat, c + 1)
                    for r in range(RPT):
                        mm = pe.transpose(tr[:, r, :], yT[:, r * P:(r + 1) * P], ident[:, :])
                    mm.then_inc(C.turned, 1)
                if (st + 1).within(TILES):
                    transpose_picked(st + 1)
                prev = st - 1

                def down(g, last):
                    if prev.within(TILES):
                        u = prev.parity
                        pe_down(pe, C, prev, g, [(dn[:, :], lambda w, f: w2[:, u, w, f * P:(f + 1) * P])], last)

                if prev.within(TILES):
                    wait(pe, s_w2[prev.parity], 16 * (prev.half + 1))
                    wait(pe, C.flat, st.value - 1)
                down(0, False)
                if st.within(TILES):
                    pe_up(pe, C, st, 1, w1[:, st.parity, :, :])
                down(1, True)

            transpose_picked(Step(0, 0))
            run_steps(pe, TILES, step_c)


def kernel(x, itok_B_0_15, L0_cond_fc1_w, L0_cond_fc1_b, L0_cond_fc2_w, L0_cond_fc2_b,
           L0_cond_experts_w, L0_cond_experts_b, L0_ffn_router_w, L0_ffn_expert_w1, L0_ffn_expert_w2):
    import numpy as np
    import concourse.bacc as bacc
    from concourse.bass_utils import run_bass_kernel_spmd

    x = np.ascontiguousarray(x)
    arrays = {
        "xT": x.reshape(TOKENS, P).T,
        "x": x,
        "itok": np.asarray(itok_B_0_15).reshape(1, SEQS),
        "fc1T": np.asarray(L0_cond_fc1_w).T,
        "fc1_b": np.asarray(L0_cond_fc1_b).reshape(FB, P).T,
        "fc2T": np.asarray(L0_cond_fc2_w).reshape(SHARED, FB, P).transpose(2, 1, 0),
        "fc2_b": np.asarray(L0_cond_fc2_b).reshape(SHARED, 1),
        "cexpT": np.asarray(L0_cond_experts_w).reshape(CEXP, PART, FB, P).transpose(0, 3, 2, 1)
                   .reshape(CEXP, P, FB * PART),
        "cexp_b": np.asarray(L0_cond_experts_b),
        "routerT": np.asarray(L0_ffn_router_w).T,
        "w1T": np.asarray(L0_ffn_expert_w1).transpose(2, 0, 1),
        "w2T": np.asarray(L0_ffn_expert_w2).reshape(EXP, P, FB, P).transpose(3, 0, 2, 1).reshape(P, EXP, HID),
    }
    arrays = {"in_" + k: np.ascontiguousarray(v) for k, v in arrays.items()}
    nc = bacc.Bacc("TRN2", target_bir_lowering=False, num_devices=1)
    args = [nc.dram_tensor(k, v.shape, mybir.dt.from_np(v.dtype), kind="ExternalInput").ap()
            for k, v in arrays.items()]
    out = nc.dram_tensor("out", (SEQS, P, P), F32, kind="ExternalOutput").ap()
    build(nc, *args, out)
    r = run_bass_kernel_spmd(nc, [arrays], core_ids=[0])
    return r.results[0]["out"]
```

```python
from contextlib import ExitStack

import concourse.bass as bass
from concourse import mybir

F32 = mybir.dt.float32
F32R = mybir.dt.float32r
BF16 = mybir.dt.bfloat16
I32 = mybir.dt.int32
ALU = mybir.AluOpType
ACT = mybir.ActivationFunctionType
AX = mybir.AxisListType.X

P = 128
SEQS = 32
TOKENS = SEQS * P
HID = 512
FB = HID // P
GB = FB // 2
PART = 32
SHARED = P - PART
CEXP = 16
EXP = 8
TOPK = 2
TILE = 512
RPT = TILE // P
CHUNKS = TOKENS // TILE
UNIT = TILE // 2
ROOM = TOKENS // UNIT + 1
MAXU = TOKENS // UNIT
FILL_UNIT = EXP * ROOM
LEAD = 8
NARROW = 8
WIDE = LEAD + NARROW
TILES = WIDE + NARROW
assert (TOPK * TOKENS + EXP * (UNIT - 1)) // UNIT <= 2 * WIDE + NARROW and NARROW >= EXP
ROW = P + 4
NO_ROW = 1 << 24
POOL_EXP = EXP // 2
LAG = 2
FIN_GROUP = 4
GROUPS = SEQS // FIN_GROUP
MISC_RANK, MISC_TOTAL = 64, 96


class Step:

    def __init__(self, pair, offset, lead=False):
        self.pair, self.offset, self.lead = pair, offset, lead
        self.value = 2 * pair + offset
        self.parity = offset % 2
        self.half = pair + offset // 2

    def __add__(self, d):
        return Step(self.pair, self.offset + d, self.lead)

    def __sub__(self, d):
        return self + (-d)

    def is_step(self, n):
        return isinstance(self.value, int) and self.value == n

    def within(self, n):
        return not isinstance(self.value, int) or 0 <= self.value < n

    def leads(self):
        return self.value < LEAD if isinstance(self.value, int) else self.lead

    def blocks(self):
        return RPT if self.leads() or self.parity == 0 else RPT // 2

    def entry(self):
        if self.leads():
            return self.value
        return self.half + LEAD // 2 if self.parity == 0 else self.half + WIDE - LEAD // 2

    def blocks_upto(self):
        if self.leads() or self.parity == 0:
            return RPT * (self.half + 1)
        return RPT * (LEAD // 2) + RPT // 2 * (self.half + 1 - LEAD // 2)


def wait(eng, sem, value):
    if not isinstance(value, int) or value > 0:
        eng.wait_ge(sem, value)


def run_steps(eng, n, body, ahead=1):
    pairs = (n - ahead - LAG) // 2
    for s in range(LAG):
        body(Step(0, s))
    with eng.Fori(1, 1 + pairs) as i:
        body(Step(i, 0))
        body(Step(i, 1))
    for s in range(LAG + 2 * pairs, n + LAG):
        body(Step(s // 2, s % 2))


def run_tiles(eng, body):
    for s in range(LAG):
        body(Step(0, s))
    with eng.Fori(1, LEAD // 2 - 1) as i:
        body(Step(i, 0, lead=True))
        body(Step(i, 1, lead=True))
    for s in range(LEAD - 2, LEAD + LAG):
        body(Step(s // 2, s % 2))
    with eng.Fori((LEAD + LAG) // 2, TILES // 2 - 1) as i:
        body(Step(i, 0))
        body(Step(i, 1))
    for s in range(TILES - 2, TILES + LAG):
        body(Step(s // 2, s % 2))


def run_pairs(eng, n, body):
    body(Step(0, 0))
    body(Step(0, 1))
    with eng.Fori(1, n // 2) as i:
        body(Step(i, 0))
        body(Step(i, 1))
    if n % 2:
        body(Step(n // 2, 0))


def build(nc, xT, x, itok, fc1T, fc1_b, fc2T, fc2_b, cexpT, cexp_b, routerT, w1T, w2T, out):
    assert LAG == 2
    slots = nc.dram_tensor("slots", ((FILL_UNIT + 2) * UNIT, ROW), F32, kind="Internal").ap()
    results = nc.dram_tensor("results", (TOPK * TOKENS, P), F32, kind="Internal").ap()
    result_groups = results.rearrange("(k p g s) d -> p k g (s d)", k=TOPK, p=P, g=GROUPS)
    x_all = x.rearrange("s p d -> p s d")
    out_store = out.rearrange("s p d -> p s d")

    with ExitStack() as ctx:
        def sb(name, shape, dt=F32):
            return ctx.enter_context(nc.sbuf_tensor(name, shape, dt))

        def ps(name, shape):
            return ctx.enter_context(nc.psum_tensor(name, shape, F32))

        def sem(name):
            return ctx.enter_context(nc.semaphore(name))

        fc1_raw = sb("fc1_raw", [P, HID])
        fc1 = sb("fc1", [P, 2, HID], F32R)
        fc2_raw = sb("fc2_raw", [P, FB, SHARED])
        fc2 = sb("fc2", [P, 2, FB, SHARED], F32R)
        cexp_raw = sb("cexp_raw", [P, 2, RPT, FB, PART])
        cexp = sb("cexp", [P, 2, 2, FB, RPT, PART], F32R)
        ffn_raw = sb("ffn_raw", [P, 2 * HID])
        ffn = sb("ffn", [P, EXP, 2, 2, HID], F32R)
        z_rows = ffn[:, :, :, :, :].rearrange("p e w h n -> p (e w h n)").bitcast(F32)[:, 0:GROUPS * TOPK * TILE]\
            .rearrange("p (g k n) -> p g k n", g=GROUPS, k=TOPK)
        w1 = sb("w1", [P, 2, 2, HID], F32R)
        w2 = sb("w2", [P, 2, 2, HID], F32R)
        router = sb("router", [P, EXP])
        fc1_bias = sb("fc1_bias", [P, FB])
        fc2_bias = sb("fc2_bias", [SHARED, 1])
        cexp_bias = sb("cexp_bias", [CEXP, PART])
        seq_bias = sb("seq_bias", [P, SEQS])
        x_raw = sb("x_raw", [P, 2, TILE])
        xs = sb("xs", [P, 2, 2, TILE], F32R)
        hid = sb("hid", [P, 2, GB * TILE])
        hs = sb("hs", [P, 2, 2, 2, GB * TILE], F32R)
        yT = sb("yT", [P, TILE])
        y_rows = sb("y_rows", [P, 2, TOPK, RPT, ROW])
        rows = sb("rows", [P, 2, RPT, P])
        picked = sb("picked", [P, 2, RPT, ROW])
        filler = sb("filler", [P, RPT, ROW])
        x_rows = sb("x_rows", [P, SEQS, P])
        pool_raw = x_rows[:, :, :].rearrange("p s d -> p (s d)").rearrange("p (e w n) -> p e w n", e=POOL_EXP, w=2)
        ident = sb("ident", [P, P])
        ones_b = sb("ones_b", [P, P], BF16)
        before = sb("before", [P, P], BF16)
        part_i = sb("part_i", [CEXP, 1], I32)
        part_f = sb("part_f", [CEXP, 1])
        exp_i = sb("exp_i", [P, EXP], I32)
        exp_f = sb("exp_f", [P, EXP])
        room_i = sb("room_i", [P, EXP], I32)
        room = sb("room", [P, EXP])
        fill_i = sb("fill_i", [P, MAXU], I32)
        fill = sb("fill", [P, MAXU])
        tile_i = sb("tile_i", [P, TILES], I32)
        tile_f = sb("tile_f", [P, TILES])
        units_i = sb("units_i", [P, TILES], I32)
        units_f = sb("units_f", [P, TILES])
        carry_i = sb("carry_i", [P, EXP, RPT + 1], I32)
        carry = sb("carry", [P, EXP, RPT + 1])
        result_row = sb("result_row", [P, CHUNKS, TOPK, RPT], I32)
        ones_f = sb("ones_f", [P, EXP])
        warm = sb("warm", [P, 1])
        itok_row = sb("itok_row", [1, SEQS], I32)
        itok_all = sb("itok_all", [CEXP, SEQS], I32)
        itok_f = sb("itok_f", [CEXP, SEQS])
        seq_hot = sb("seq_hot", [CEXP, SEQS])
        top = sb("top", [P, RPT, EXP])
        top_exp = sb("top_exp", [P, RPT, EXP], mybir.dt.uint32)
        chosen = sb("chosen", [P, RPT, TOPK, EXP], BF16)
        either = sb("either", [P, RPT, EXP], BF16)
        run = sb("run", [P, EXP, RPT + 1])
        base = sb("base", [P, EXP, RPT + 1])
        place = sb("place", [P, RPT, EXP])
        place_c = sb("place_c", [P, RPT, TOPK, EXP])
        slot_f = sb("slot_f", [P, RPT * TOPK])
        slot = sb("slot", [P, 2, RPT * TOPK], I32)
        gap = sb("gap", [P, SEQS])
        egap = sb("egap", [P, SEQS])
        denom = sb("denom", [P, SEQS])
        gate = sb("gate", [P, TOPK, SEQS])
        count = sb("count", [P, EXP])
        over = sb("over", [P, EXP, MAXU])
        units = sb("units", [P, EXP])
        pairs_of = sb("pairs_of", [P, EXP])
        pairs_upto = sb("pairs_upto", [P, EXP])
        pairs_left = sb("pairs_left", [P, EXP])
        wide_max = sb("wide_max", [P, EXP])
        wide_run = sb("wide_run", [P, EXP + 1])
        odd = sb("odd", [P, EXP])
        odd_upto = sb("odd_upto", [P, EXP])
        jump_wide = sb("jump_wide", [P, EXP])
        jump_room = sb("jump_room", [P, EXP])
        jump_step = sb("jump_step", [P, EXP])
        jump_odd = sb("jump_odd", [P, EXP])
        first_odd = sb("first_odd", [P, 1])
        passed = sb("passed", [P, TILES, EXP])
        skipped = sb("skipped", [P, TILES, EXP])
        owner_f = sb("owner_f", [P, TILES])
        owner_i = sb("owner_i", [P, TILES], I32)
        where_f = sb("where_f", [P, TILES])
        where_t = sb("where_t", [P, TILES])
        where_i = sb("where_i", [P, TILES], I32)
        end_i = sb("end_i", [P, EXP], I32)
        back = sb("back", [P, TILES, RPT], I32)
        back_now = sb("back_now", [P, 2, RPT], I32)

        hp = ps("hp", [P, 2, GB * TILE])
        dn = ps("dn", [P, TILE])
        dx = ps("dx", [P, TILE])
        tr = ps("tr", [P, RPT, P])
        misc = ps("misc", [P, TILE])

        s_const = sem("s_const")
        s_constf = sem("s_constf")
        s_load = [sem(f"s_load{n}") for n in range(9)]
        s_xrows = sem("s_xrows")
        s_xin = [sem(f"s_xin{n}") for n in range(2)]
        s_cexp = [sem(f"s_cexp{n}") for n in range(2)]
        s_pool_w = [sem(f"s_pool_w{n}") for n in range(2)]
        s_pool_hi, s_pool_lo = sem("s_pool_hi"), sem("s_pool_lo")
        s_ffn, s_ffn_hi, s_ffn_lo = sem("s_ffn"), sem("s_ffn_hi"), sem("s_ffn_lo")
        s_fc_hi, s_fc_lo = sem("s_fc_hi"), sem("s_fc_lo")
        s_hot, s_bias, s_biasc = sem("s_hot"), sem("s_bias"), sem("s_biasc")
        s_chi, s_clo = sem("s_chi"), sem("s_clo")
        s_chain = sem("s_chain")
        s_route = sem("s_route")
        s_either, s_ranked = sem("s_either"), sem("s_ranked")
        s_slot = sem("s_slot")
        s_spread = [sem(f"s_spread{n}") for n in range(2)]
        s_yfree, s_zfree = sem("s_yfree"), sem("s_zfree")
        s_gap, s_exp = sem("s_gap"), sem("s_exp")
        s_end, s_where = sem("s_end"), sem("s_where")
        s_filler, s_fillout = sem("s_filler"), sem("s_fillout")
        s_go, s_sp_go, s_dve_go, s_act_go = (sem(n) for n in ("s_go", "s_sp_go", "s_dve_go", "s_act_go"))
        s_pick = [sem(f"s_pick{n}") for n in range(2)]
        s_w1 = [sem(f"s_w1{n}") for n in range(2)]
        s_w2 = [sem(f"s_w2{n}") for n in range(2)]
        s_back = sem("s_back")
        s_zout = [sem(f"s_zout{n}") for n in range(2)]
        s_z = [sem(f"s_z{n}") for n in range(GROUPS)]
        s_gate = sem("s_gate")
        s_half, s_second, s_fin = sem("s_half"), sem("s_second"), sem("s_fin")
        s_out = sem("s_out")

        class Counts:

            def __init__(self, tag, per_group, width):
                self.per = per_group
                self.width = width
                self.xhi = sem(tag + "xhi")
                self.xlo = sem(tag + "xlo")
                self.up = sem(tag + "up")
                self.gelu = sem(tag + "gelu")
                self.hi = sem(tag + "hi")
                self.lo = sem(tag + "lo")
                self.down = sem(tag + "down")
                self.flat = sem(tag + "flat")
                self.flat2 = sem(tag + "flat2")
                self.turned = sem(tag + "turned")
                self.rows = sem(tag + "rows")
                self.rows2 = sem(tag + "rows2")
                self.tin = sem(tag + "tin")
                self.score = sem(tag + "score")

        A = Counts("a_", GB, lambda st: TILE)
        C = Counts("c_", 1, lambda st: st.blocks() * P)

        def by_block(k, st, group):
            width = k.width(st)
            if width == TILE:
                return group
            return group.rearrange("p (n t) -> p n t", t=TILE)[:, :, 0:width]

        def pe_up(pe, k, st, g, weight):
            wait(pe, k.gelu, 2 * k.per * (st.value - 1) + k.per * (g + 1))
            width = k.width(st)
            for n in range(GB):
                cols = slice((g * GB + n) * P, (g * GB + n + 1) * P)
                dst = hp[:, g, n * TILE:n * TILE + width]
                passes = [(0, 1), (1, 0), (0, 0)]
                for m, (w, v) in enumerate(passes):
                    mm = pe.matmul(dst, weight[:, w, cols], xs[:, st.parity, v, 0:width],
                                   start=m == 0, stop=m == len(passes) - 1)
                if k.per == GB or n == GB - 1:
                    mm.then_inc(k.up, 1)

        def pe_down(pe, k, st, g, products, last_inc, between=None):
            wait(pe, k.lo, 2 * st.value + g + 1)
            width = k.width(st)
            for dst, weight in products:
                for n in range(GB):
                    f = g * GB + n
                    for m, (w, v) in enumerate([(0, 1), (1, 0), (0, 0)]):
                        mm = pe.matmul(dst, weight(w, f), hs[:, st.parity, v, g, n * TILE:n * TILE + width],
                                       start=(f == 0 and m == 0), stop=(f == FB - 1 and m == 2))
                if between and dst is products[0][0]:
                    between()
            if last_inc:
                mm.then_inc(k.down, 1)

        def act_gelu(act, k, st, g, bias):
            wait(act, k.lo, 2 * (st.value - 1) + g + 1)
            n_per = GB // k.per
            for n in range(k.per):
                wait(act, k.up, 2 * k.per * st.value + k.per * g + n + 1)
                cols = slice(n * n_per * TILE, (n + 1) * n_per * TILE)
                if bias is None:
                    ins = act.activation(by_block(k, st, hid[:, g, :]), by_block(k, st, hp[:, g, :]), ACT.Gelu)
                else:
                    f = g * GB + n
                    ins = act.activation(hid[:, g, cols], hp[:, g, cols], ACT.Gelu, bias=bias[:, f:f + 1])
                ins.then_inc(k.gelu, 1)

        def act_high(act, k, st, g):
            wait(act, k.gelu, 2 * k.per * st.value + k.per * (g + 1))
            wait(act, k.down, st.value - 1)
            act.activation(by_block(k, st, hs[:, st.parity, 0, g, :]), by_block(k, st, hid[:, g, :]), ACT.Copy)\
               .then_inc(k.hi, 1)

        def act_hidden(act, k, st, g, bias):
            act_gelu(act, k, st, g, bias)
            act_high(act, k, st, g)

        def dve_hidden(dve, k, st, g):
            wait(dve, k.hi, 2 * st.value + g + 1)
            dve.tensor_tensor(by_block(k, st, hs[:, st.parity, 1, g, :]), by_block(k, st, hid[:, g, :]),
                              by_block(k, st, hs[:, st.parity, 0, g, :].bitcast(F32)), ALU.subtract)\
               .then_inc(k.lo, 1)

        def first_slot(eng, st):
            return eng.value_load(where_i[0:1, bass.ds(st.entry(), 1)], min_val=0, max_val=FILL_UNIT * UNIT)

        def load_picked(eng, st, row):
            eng.dma_start(picked[:, st.parity, 0:st.blocks(), :].rearrange("p r w -> p (r w)"),
                         slots[bass.ds(row, st.blocks() * P), :].rearrange("(p r) w -> p (r w)", p=P))\
              .then_inc(s_pick[st.parity], 16)

        def write_fillers(eng, experts):
            eng.wait_ge(s_end, 1)
            eng.wait_ge(s_filler, 2)
            for e in experts:
                row = eng.value_load(end_i[0:1, e:e + 1], min_val=e * ROOM * UNIT,
                                     max_val=e * ROOM * UNIT + TOKENS)
                eng.dma_start(slots[bass.ds(row, UNIT), :].rearrange("(p r) w -> p (r w)", p=P),
                              filler[:, 0:UNIT // P, :].rearrange("p r w -> p (r w)")).then_inc(s_fillout, 16)

        block_ctx = ctx.enter_context(nc.Block())

        @block_ctx.sync
        def _(sp):
            sp.dma_start(x_raw[:, 0, :], xT[:, 0:TILE]).then_inc(s_xin[0], 16)
            sp.dma_start(fc1_raw[:, :], fc1T).then_inc(s_load[1], 16)
            sp.dma_start(fc1_bias[:, :], fc1_b).then_inc(s_load[2], 16)
            sp.dma_start(fc2_raw[:, :, :], fc2T).then_inc(s_load[3], 16)
            sp.dma_start(x_raw[:, 1, :], xT[:, TILE:2 * TILE]).then_inc(s_xin[1], 16)
            sp.dma_start(itok_row[:, :], itok).then_inc(s_load[0], 16)
            sp.dma_start(itok_all[:, :], itok.to_broadcast((CEXP, SEQS))).then_inc(s_load[5], 16)
            sp.dma_start(cexp_bias[:, :], cexp_b).then_inc(s_load[6], 16)
            sp.dma_start(fc2_bias[:, :], fc2_b).then_inc(s_load[4], 16)
            sp.dma_start(router[:, :], routerT).then_inc(s_load[7], 16)

            def load_x(st):
                c, u = st.value, st.parity
                wait(sp, A.xlo, c - 1)
                sp.dma_start(x_raw[:, u, :], xT[:, bass.ds(c * TILE, TILE)]).then_inc(s_xin[u], 16)

            def load_cexp(st):
                c, u = st.value, st.parity
                wait(sp, s_clo, c - 1)
                sp.wait_ge(s_load[0], 16)
                sp.sem_inc(s_sp_go, 1)
                for r in range(RPT):
                    e = sp.value_load(itok_row[0:1, bass.ds(c * RPT + r, 1)], min_val=0, max_val=CEXP - 1)
                    sp.dma_start(cexp_raw[:, u, r, :, :].rearrange("p f c -> p (f c)"),
                                 cexpT[bass.ds(e, 1), :, :].rearrange("e p n -> p (e n)"))\
                      .then_inc(s_cexp[u], 16)

            def step_a(st):
                if (st + 2).within(CHUNKS):
                    load_x(st + 2)
                if (st + 1).within(CHUNKS):
                    load_cexp(st + 1)
                if st.parity == 0 and (st + 1).within(CHUNKS):
                    e = POOL_EXP + st.half
                    wait(sp, s_ffn_lo, st.half)
                    for n, w in enumerate((w1T, w2T)):
                        sp.dma_start(ffn_raw[:, n * HID:(n + 1) * HID],
                                     w[:, bass.ds(e, 1), :].rearrange("p e n -> p (e n)")).then_inc(s_ffn, 16)
                if st.is_step(0):
                    for h in range(2):
                        half = slice(h * POOL_EXP // 2, (h + 1) * POOL_EXP // 2)
                        for n, w in enumerate((w1T, w2T)):
                            sp.dma_start(pool_raw[:, half, n, :], w[:, half, :]).then_inc(s_pool_w[h], 16)

            load_cexp(Step(0, 0))
            run_steps(sp, CHUNKS, step_a, ahead=2)
            sp.wait_ge(s_pool_lo, POOL_EXP)
            sp.dma_start(x_rows[:, :, :], x_all).then_inc(s_xrows, 16)
            sp.wait_ge(s_filler, 2)
            sp.dma_start(slots[FILL_UNIT * UNIT:(FILL_UNIT + 2) * UNIT, :].rearrange("(p r) w -> p (r w)", p=P),
                         filler[:, :, :].rearrange("p r w -> p (r w)"))\
              .then_inc(s_fillout, 16)

            def load_weights(st, which, dst, sems):
                sp.sem_inc(s_sp_go, 1)
                e = sp.value_load(owner_i[0:1, bass.ds(st.entry(), 1)], min_val=0, max_val=EXP - 1)
                sp.dma_start(dst[:, st.parity, :, :].rearrange("p h n -> p (h n)").bitcast(F32),
                             ffn[:, bass.ds(e, 1), which, :, :].rearrange("p e h n -> p (e h n)").bitcast(F32))\
                  .then_inc(sems[st.parity], 16)

            def step_c(st):
                if (st + 1).within(TILES):
                    wait(sp, C.up, 2 * st.value)
                    load_weights(st + 1, 0, w1, s_w1)
                if st.within(TILES):
                    wait(sp, C.down, st.value - 1)
                    load_weights(st, 1, w2, s_w2)

            write_fillers(sp, range(EXP // 2))
            sp.wait_ge(s_where, 1)
            sp.wait_ge(s_pool_lo, POOL_EXP)
            sp.wait_ge(s_ffn_lo, EXP - POOL_EXP)
            load_weights(Step(0, 0), 0, w1, s_w1)
            first_rows = [first_slot(sp, Step(0, s)) for s in range(2)]
            sp.wait_ge(s_fillout, 16 * (EXP + 1))
            for u in range(2):
                sp.wait_ge(s_spread[u], 16 * RPT * TOPK * (CHUNKS // 2))
            for s in range(2):
                load_picked(sp, Step(0, s), first_rows[s])
            run_tiles(sp, step_c)

            for u in range(2):
                sp.wait_ge(s_zout[u], 16 * Step(TILES // 2 - 1, u).blocks_upto())

            def load_z(g):
                for k in range(TOPK):
                    sp.dma_start(z_rows[:, g, k, :], result_groups[:, k, g, :])\
                      .then_inc(s_z[g], 16)

            for g in range(GROUPS):
                load_z(g)
            for g in range(GROUPS):
                sp.wait_ge(s_fin, g + 1)
                sp.dma_start(out_store[:, g * FIN_GROUP:(g + 1) * FIN_GROUP, :],
                             z_rows[:, g, 0, :].rearrange("p (s d) -> p s d", d=P)).then_inc(s_out, 16)
            sp.wait_ge(s_out, 16 * GROUPS)

        @block_ctx.gpsimd
        def _(pool):
            pool.sem_inc(s_yfree, 2)
            pool.sem_inc(s_zfree, 2)
            pool.memset(ones_f[:, :], 1.0).then_inc(s_const, 1)
            pool.memset(ident[:, :], 1.0).then_inc(s_const, 1)
            pool.memset(before[:, :], 1.0).then_inc(s_const, 1)
            pool.memset(ones_b[:, :], 1.0).then_inc(s_const, 1)
            pool.memset(filler[:, :, :], 0.0).then_inc(s_filler, 1)
            pool.memset(y_rows[:, :, :, :, P:ROW], 0.0).then_inc(s_const, 1)
            pool.iota(part_i[:, :], [[0, 1]], base=0, channel_multiplier=1).then_inc(s_const, 1)
            pool.iota(exp_i[:, :], [[1, EXP]], base=0, channel_multiplier=0).then_inc(s_const, 1)
            pool.iota(room_i[:, :], [[ROOM * UNIT, EXP]], base=0, channel_multiplier=0).then_inc(s_const, 1)
            pool.iota(fill_i[:, :], [[UNIT, MAXU]], base=0, channel_multiplier=0).then_inc(s_const, 1)
            for n, entries in enumerate((slice(0, WIDE), slice(WIDE, TILES))):
                size = entries.stop - entries.start
                pool.iota(tile_i[:, entries], [[1, size]], base=0, channel_multiplier=0).then_inc(s_const, 1)
                pool.iota(units_i[:, entries], [[2 - n, size]], base=0, channel_multiplier=0).then_inc(s_const, 1)
            pool.iota(carry_i[:, :, :], [[0, EXP], [1, RPT + 1]], base=0, channel_multiplier=0)\
                .then_inc(s_const, 1)
            pool.iota(result_row[:, :, :, :], [[RPT, CHUNKS], [TOKENS, TOPK], [1, RPT]], base=0,
                      channel_multiplier=SEQS).then_inc(s_const, 1)
            pool.wait_ge(s_const, 15)
            pool.affine_select(out=ident[:, :], in_=ident[:, :], compare_op=ALU.is_equal, fill=0.0,
                               base=0, pattern=[[-1, P]], channel_multiplier=1).then_inc(s_const, 1)
            pool.affine_select(out=before[:, :], in_=before[:, :], compare_op=ALU.is_gt, fill=0.0,
                               base=0, pattern=[[1, P]], channel_multiplier=-1).then_inc(s_const, 1)
            pool.wait_ge(s_filler, 1)
            pool.memset(filler[:, :, P:P + 1].bitcast(I32), NO_ROW).then_inc(s_filler, 1)

            with pool.Fori(0, POOL_EXP) as e:
                hi = ffn[:, bass.ds(e, 1), :, 0, :].rearrange("p e w n -> p (e w) n")
                lo = ffn[:, bass.ds(e, 1), :, 1, :].rearrange("p e w n -> p (e w) n")
                raw = pool_raw[:, bass.ds(e, 1), :, :].rearrange("p e w n -> p (e w) n")
                wait(pool, s_pool_hi, e + 1)
                pool.tensor_tensor(lo, raw, hi.bitcast(F32), ALU.subtract).then_inc(s_pool_lo, 1)

            def free_rows(before, sems, scatters, free):
                if not isinstance(before.value, int) or before.value >= 0:
                    wait(pool, sems[before.parity], 16 * scatters)
                    pool.sem_inc(free, 1)

            def spread(st):
                c, u = st.value, st.parity
                wait(pool, A.rows, c + 1)
                wait(pool, A.rows2, c + 1)
                wait(pool, s_slot, c + 1)
                pool.sem_inc(s_go, 1)
                for r in range(RPT):
                    if r == RPT // 2:
                        free_rows(st - 1, s_spread, TOPK * RPT * ((st - 1).half + 1), s_yfree)
                        pool.sem_inc(s_go, 1)
                    for k in range(TOPK):
                        n = r * TOPK + k
                        pool.indirect_dma_start(
                            out=slots, out_offset=bass.IndirectOffsetOnAxis(ap=slot[:, u, n:n + 1], axis=0),
                            in_=y_rows[:, u, k, r, :], in_offset=None).then_inc(s_spread[u], 16)

            run_pairs(pool, CHUNKS, spread)

            def send_back(st):
                t, u = st.value, st.parity
                wait(pool, C.rows, t + 1)
                blocks = st.blocks()
                pool.tensor_copy(back_now[:, u, 0:blocks], back[:, bass.ds(t, 1), 0:blocks].rearrange("p t r -> p (t r)"))\
                    .then_inc(s_back, 1)
                wait(pool, s_back, t + 1)
                pool.sem_inc(s_go, 1)
                for r in range(st.blocks()):
                    if r == st.blocks() // 2:
                        free_rows(st - 1, s_zout, (st - 1).blocks_upto(), s_zfree)
                        pool.sem_inc(s_go, 1)
                    pool.indirect_dma_start(
                        out=results, out_offset=bass.IndirectOffsetOnAxis(ap=back_now[:, u, r:r + 1], axis=0),
                        in_=rows[:, u, r, :], in_offset=None,
                        bounds_check=TOPK * TOKENS - 1, oob_is_err=False).then_inc(s_zout[u], 16)

            send_back(Step(0, 0))
            send_back(Step(0, 1))
            with pool.Fori(1, LEAD // 2) as i:
                send_back(Step(i, 0, lead=True))
                send_back(Step(i, 1, lead=True))
            send_back(Step(LEAD // 2, 0))
            send_back(Step(LEAD // 2, 1))
            with pool.Fori(LEAD // 2 + 1, TILES // 2) as i:
                send_back(Step(i, 0))
                send_back(Step(i, 1))

            def add_second(g):
                wait(pool, s_half, g + 1)
                wait(pool, s_second, g + 1)
                z0, z1 = (z_rows[:, g, k, :] for k in range(TOPK))
                pool.tensor_tensor(z0, z0, z1, ALU.add).then_inc(s_fin, 1)

            for g in range(GROUPS):
                add_second(g)

        @block_ctx.scalar
        def _(act):
            act.wait_ge(s_const, 1)
            act.activation(warm[:, :], ones_f[:, 0:1], ACT.Gelu)
            act.wait_ge(s_load[1], 16)
            act.activation(fc1[:, 0, :], fc1_raw[:, :], ACT.Copy).then_inc(s_fc_hi, 1)

            def split_x(st):
                wait(act, s_xin[st.parity], 16 * st.half + 16)
                act.activation(xs[:, st.parity, 0, :], x_raw[:, st.parity, :], ACT.Copy).then_inc(A.xhi, 1)

            split_x(Step(0, 0))
            act.wait_ge(s_load[3], 16)
            act.activation(fc2[:, 0, :, :], fc2_raw[:, :, :], ACT.Copy).then_inc(s_fc_hi, 1)
            act.wait_ge(s_load[2], 16)

            def staged_high(h):
                wait(act, s_pool_w[h], 32)
                for e in range(h * POOL_EXP // 2, (h + 1) * POOL_EXP // 2):
                    act.activation(ffn[:, e, :, 0, :], pool_raw[:, e, :, :], ACT.Copy).then_inc(s_pool_hi, 1)

            def step_a(st):
                if st.is_step(0):
                    split_x(st + 1)
                if st.within(CHUNKS):
                    act_gelu(act, A, st, 0, fc1_bias)
                if (st - 2).within(CHUNKS):
                    done = st - 2
                    wait(act, A.turned, done.value + 1)
                    wait(act, A.rows, done.value + 1)
                    act.activation(y_rows[:, done.parity, 1, :, 0:P], tr[:, :, :], ACT.Copy)\
                       .then_inc(A.rows2, 1)
                if st.within(CHUNKS):
                    if (st + 1).within(CHUNKS) and not st.is_step(0):
                        split_x(st + 1)
                    if st.is_step(0):
                        act_high(act, A, st, 0)
                    wait(act, s_cexp[st.parity], 16 * RPT * (st.half + 1))
                    act.activation(cexp[:, st.parity, 0, :, :, :],
                                   cexp_raw[:, st.parity, :, :, :].rearrange("p r f c -> p f r c"),
                                   ACT.Copy).then_inc(s_chi, 1)
                    if not st.is_step(0):
                        act_high(act, A, st, 0)
                    if st.parity == 1:
                        wait(act, s_ffn, 32 * (st.half + 1))
                        act.activation(ffn[:, bass.ds(POOL_EXP + st.half, 1), :, 0, :]
                                       .rearrange("p e w n -> p (e w) n"),
                                       ffn_raw[:, :].rearrange("p (w n) -> p w n", w=2), ACT.Copy)\
                           .then_inc(s_ffn_hi, 1)
                    act_hidden(act, A, st, 1, fc1_bias)
                if (st - 1).within(CHUNKS):
                    c = (st - 1).value
                    wait(act, A.down, c + 1)
                    wait(act, A.score, c)
                    act.activation(yT[0:SHARED, :], dn[0:SHARED, :], ACT.Identity, bias=fc2_bias[:, 0:1])\
                       .then_inc(A.flat2, 1)
                    if st.is_step(1):
                        for h in range(2):
                            staged_high(h)

            act.wait_ge(s_load[4], 16)
            run_steps(act, CHUNKS, step_a)

            write_fillers(act, range(EXP // 2, EXP))
            act.wait_ge(s_gap, 1)
            act.activation(egap[:, :], gap[:, :], ACT.Exp).then_inc(s_exp, 1)
            act.activation(warm[:, :], ones_f[:, 0:1], ACT.Gelu)

            def split_picked(st):
                wait(act, C.tin, st.value + 1)
                width = C.width(st)
                act.activation(xs[:, st.parity, 0, 0:width], dx[:, 0:width], ACT.Copy).then_inc(C.xhi, 1)

            def step_c(st):
                if (st + 2).within(TILES):
                    wait(act, C.xlo, st.value + 1)
                    act.sem_inc(s_act_go, 1)
                    load_picked(act, st + 2, first_slot(act, st + 2))
                if st.within(TILES):
                    act_gelu(act, C, st, 0, None)
                    if (st + 1).within(TILES):
                        split_picked(st + 1)
                    act_high(act, C, st, 0)
                    act_hidden(act, C, st, 1, None)

            split_picked(Step(0, 0))
            run_tiles(act, step_c)

            act.wait_ge(s_gate, 1)

            def scale_second(g):
                act.wait_ge(s_z[g], 16 * TOPK)
                z1 = z_rows[:, g, 1, :].rearrange("p (s d) -> p s d", d=P)
                for r in range(FIN_GROUP):
                    ins = act.activation(z1[:, r, :], z1[:, r, :], ACT.Copy,
                                         scale=gate[:, 1, g * FIN_GROUP + r:g * FIN_GROUP + r + 1])
                ins.then_inc(s_second, 1)

            for g in range(GROUPS):
                scale_second(g)

        @block_ctx.vector
        def _(dve):
            links = [0]

            def link(ins):
                links[0] += 1
                ins.then_inc(s_chain, 1)
                dve.wait_ge(s_chain, links[0])

            dve.wait_ge(s_fc_hi, 1)
            dve.tensor_tensor(fc1[:, 1, :], fc1_raw[:, :], fc1[:, 0, :].bitcast(F32), ALU.subtract)\
               .then_inc(s_fc_lo, 1)

            def split_x(st):
                wait(dve, A.xhi, st.value + 1)
                dve.tensor_tensor(xs[:, st.parity, 1, :], x_raw[:, st.parity, :],
                                  xs[:, st.parity, 0, :].bitcast(F32), ALU.subtract).then_inc(A.xlo, 1)

            split_x(Step(0, 0))
            dve.wait_ge(s_const, 17)
            dve.tensor_copy(part_f[:, :], part_i[:, :])
            dve.tensor_copy(exp_f[:, :], exp_i[:, :])
            dve.tensor_copy(room[:, :], room_i[:, :])
            dve.tensor_copy(run[:, :, 0], room_i[:, :])
            dve.tensor_copy(fill[:, :], fill_i[:, :])
            dve.tensor_copy(tile_f[:, :], tile_i[:, :])
            dve.tensor_copy(units_f[:, :], units_i[:, :])
            dve.tensor_scalar(wide_run[:, :], carry_i[:, :, :].rearrange("p e r -> p (e r)")[:, 0:EXP + 1], 0.0,
                              None, ALU.mult)
            dve.tensor_scalar(carry[:, :, :], carry_i[:, :, :], 1.0, None, ALU.min)
            dve.wait_ge(s_load[5], 16)
            link(dve.tensor_copy(itok_f[:, :], itok_all[:, :]))
            dve.tensor_scalar(seq_hot[:, :], itok_f[:, :], part_f[:, 0:1], None, ALU.is_equal)\
               .then_inc(s_hot, 1)
            dve.wait_ge(s_fc_hi, 2)
            dve.tensor_tensor(fc2[:, 1, :, :], fc2_raw[:, :, :], fc2[:, 0, :, :].bitcast(F32), ALU.subtract)\
               .then_inc(s_fc_lo, 1)

            LINKS = 8

            def linker(c):
                n = [0]

                def link_c(ins):
                    n[0] += 1
                    ins.then_inc(s_route, 1)
                    wait(dve, s_route, LINKS * c + n[0])
                return link_c, n

            def choose(st, link_c):
                dve.sem_inc(s_dve_go, 1)
                for r in range(RPT):
                    ins = dve.max(top[:, r, :], misc[:, r * EXP:(r + 1) * EXP])
                link_c(ins)
                dve.sem_inc(s_dve_go, 1)
                for r in range(RPT):
                    ins = dve.max_index(top_exp[:, r, :], top[:, r, :], misc[:, r * EXP:(r + 1) * EXP])
                link_c(ins)
                seqs = bass.ds(st.value * RPT, RPT)
                dve.tensor_tensor(gap[:, seqs], top[:, :, 1], top[:, :, 0], ALU.subtract)
                link_c(dve.tensor_tensor(
                    chosen[:, :, :, :], exp_f[:, :].unsqueeze(1).unsqueeze(1).to_broadcast((P, RPT, TOPK, EXP)),
                    top_exp[:, :, 0:TOPK].unsqueeze(3).to_broadcast((P, RPT, TOPK, EXP)), ALU.is_equal))
                dve.tensor_tensor(either[:, :, :], chosen[:, :, 0, :], chosen[:, :, 1, :], ALU.add)\
                   .then_inc(s_either, 1)

            def place_pairs(st, link_c):
                wait(dve, s_ranked, st.value + 1)
                link_c(dve.tensor_copy(run[:, :, 1:RPT + 1],
                                       misc[:, MISC_TOTAL:MISC_TOTAL + RPT * EXP]
                                       .rearrange("p (r e) -> p e r", e=EXP)))
                link_c(dve.tensor_tensor_scan(base[:, :, :].rearrange("p e r -> p (e r)"),
                                              carry[:, :, :].rearrange("p e r -> p (e r)"),
                                              run[:, :, :].rearrange("p e r -> p (e r)"), 0.0,
                                              ALU.mult, ALU.add))
                dve.tensor_copy(run[:, :, 0], base[:, :, RPT])
                link_c(dve.tensor_tensor(place[:, :, :], base[:, :, 0:RPT].rearrange("p e r -> p r e"),
                                         misc[:, MISC_RANK:MISC_RANK + RPT * EXP]
                                         .rearrange("p (r e) -> p r e", e=EXP), ALU.add))
                link_c(dve.tensor_tensor(place_c[:, :, :, :],
                                         place[:, :, :].unsqueeze(2).to_broadcast((P, RPT, TOPK, EXP)),
                                         chosen[:, :, :, :], ALU.mult))
                link_c(dve.tensor_reduce(slot_f[:, :], place_c[:, :, :, :].rearrange("p r k e -> p (r k) e"),
                                         AX, ALU.add))
                dve.tensor_copy(slot[:, st.parity, :], slot_f[:, :]).then_inc(s_slot, 1)

            def step_a(st):
                done = st - 2
                link_c, n = linker(done.value)
                if done.within(CHUNKS):
                    wait(dve, A.turned, done.value + 1)
                    wait(dve, s_yfree, done.value + 1)
                    dve.tensor_copy(y_rows[:, done.parity, :, :, P:P + 1].bitcast(I32)
                                    .rearrange("p k r w -> p (k r w)"),
                                    result_row[:, bass.ds(done.value, 1), :, :].rearrange("p c k r -> p (c k r)"))
                    dve.tensor_copy(y_rows[:, done.parity, 0, :, 0:P], tr[:, :, :]).then_inc(A.rows, 1)
                    wait(dve, A.score, done.value + 1)
                    choose(done, link_c)
                if st.within(CHUNKS):
                    if (st + 1).within(CHUNKS):
                        split_x(st + 1)
                    if st.is_step(0):
                        dve_hidden(dve, A, st, 0)
                    wait(dve, s_chi, st.value + 1)
                    dve.tensor_tensor(cexp[:, st.parity, 1, :, :, :],
                                      cexp_raw[:, st.parity, :, :, :].rearrange("p r f c -> p f r c"),
                                      cexp[:, st.parity, 0, :, :, :].bitcast(F32), ALU.subtract)\
                       .then_inc(s_clo, 1)
                if done.within(CHUNKS):
                    place_pairs(done, link_c)
                    assert n[0] == LINKS
                if st.within(CHUNKS):
                    if not st.is_step(0):
                        dve_hidden(dve, A, st, 0)
                    if st.parity == 1:
                        wait(dve, s_ffn_hi, st.half + 1)
                        e = bass.ds(POOL_EXP + st.half, 1)
                        dve.tensor_tensor(ffn[:, e, :, 1, :].rearrange("p e w n -> p (e w) n"),
                                          ffn_raw[:, :].rearrange("p (w n) -> p w n", w=2),
                                          ffn[:, e, :, 0, :].rearrange("p e w n -> p (e w) n").bitcast(F32),
                                          ALU.subtract).then_inc(s_ffn_lo, 1)
                if st.is_step(1):
                    dve.wait_ge(s_bias, 1)
                    dve.tensor_copy(seq_bias[SHARED:P, :], misc[SHARED:P, 0:SEQS]).then_inc(s_biasc, 1)
                    dve.wait_ge(s_biasc, 1)
                if (st - 1).within(CHUNKS):
                    c = (st - 1).value
                    wait(dve, A.down, c + 1)
                    wait(dve, A.score, c)
                    for r in range(RPT):
                        ins = dve.tensor_scalar(yT[SHARED:P, r * P:(r + 1) * P],
                                                dx[r * PART:(r + 1) * PART, r * P:(r + 1) * P],
                                                seq_bias[SHARED:P, bass.ds(c * RPT + r, 1)], None, ALU.add)
                    ins.then_inc(A.flat, 1)
                if st.within(CHUNKS):
                    dve_hidden(dve, A, st, 1)

            run_steps(dve, CHUNKS, step_a)

            dve.sem_inc(s_gap, 1)
            link(dve.tensor_copy(end_i[:, :], run[:, :, 0]))
            dve.sem_inc(s_end, 1)
            link(dve.tensor_tensor(count[:, :], run[:, :, 0], room[:, :], ALU.subtract))
            link(dve.tensor_tensor(over[:, :, :], count[:, :].unsqueeze(2).to_broadcast((P, EXP, MAXU)),
                                   fill[:, :].unsqueeze(1).to_broadcast((P, EXP, MAXU)), ALU.is_gt))
            dve.tensor_reduce(units[:, :], over[:, :, :], AX, ALU.add)
            link(dve.tensor_reduce(pairs_of[:, :],
                                   over[:, :, :].rearrange("p e (m two) -> p e m two", two=2)[:, :, :, 1], AX, ALU.add))
            link(dve.tensor_tensor_scan(pairs_upto[:, :], ones_f[:, :], pairs_of[:, :], 0.0, ALU.mult, ALU.add))
            link(dve.tensor_tensor(pairs_left[:, :], pairs_of[:, :], pairs_upto[:, :], ALU.subtract))
            link(dve.scalar_tensor_tensor(wide_max[:, :], pairs_left[:, :], float(WIDE), pairs_of[:, :],
                                          ALU.add, ALU.min))
            link(dve.tensor_scalar(wide_run[:, 0:EXP], wide_max[:, :], 0.0, None, ALU.max))
            link(dve.scalar_tensor_tensor(odd[:, :], wide_run[:, 0:EXP], -2.0, units[:, :], ALU.mult, ALU.add))
            link(dve.tensor_tensor_scan(odd_upto[:, :], ones_f[:, :], odd[:, :], 0.0, ALU.mult, ALU.add))
            for entries, upto in ((slice(0, WIDE), pairs_upto), (slice(WIDE, TILES), odd_upto)):
                shape = (P, entries.stop - entries.start, EXP)
                link(dve.tensor_tensor(passed[:, entries, :], tile_f[:, entries].unsqueeze(2).to_broadcast(shape),
                                       upto[:, :].unsqueeze(1).to_broadcast(shape), ALU.is_ge))
            dve.tensor_reduce(owner_f[:, :], passed[:, :, :], AX, ALU.add)
            dve.tensor_scalar(jump_wide[:, :], pairs_of[:, :], -2.0, float(ROOM), ALU.mult, ALU.add)
            dve.tensor_scalar(jump_room[:, :], odd[:, :], -1.0, float(ROOM), ALU.mult, ALU.add)
            dve.tensor_scalar(first_odd[:, :], wide_run[:, 0:1], 2.0, None, ALU.mult)
            link(dve.tensor_tensor(jump_step[:, :], wide_run[:, 1:EXP + 1], wide_run[:, 0:EXP], ALU.subtract))
            link(dve.scalar_tensor_tensor(jump_odd[:, :], jump_step[:, :], 2.0, jump_room[:, :],
                                          ALU.mult, ALU.add))
            for entries, jump in ((slice(0, WIDE), jump_wide), (slice(WIDE, TILES), jump_odd)):
                shape = (P, entries.stop - entries.start, EXP)
                link(dve.tensor_tensor(skipped[:, entries, :], passed[:, entries, :],
                                       jump[:, :].unsqueeze(1).to_broadcast(shape), ALU.mult))
            link(dve.tensor_reduce(where_f[:, :], skipped[:, :, :], AX, ALU.add))
            dve.tensor_tensor(where_t[:, 0:WIDE], where_f[:, 0:WIDE], units_f[:, 0:WIDE], ALU.add)
            link(dve.scalar_tensor_tensor(where_t[:, WIDE:TILES], where_f[:, WIDE:TILES], first_odd[:, 0:1],
                                          units_f[:, WIDE:TILES], ALU.add, ALU.add))
            dve.tensor_scalar(where_i[:, :], where_t[:, :], float(FILL_UNIT), float(UNIT), ALU.min, ALU.mult)
            dve.tensor_scalar(owner_i[:, :], owner_f[:, :], float(EXP - 1), None, ALU.min).then_inc(s_where, 1)

            dve.wait_ge(s_exp, 1)
            link(dve.tensor_scalar(denom[:, :], egap[:, :], 1.0, None, ALU.add))
            link(dve.reciprocal(gate[:, 0, :], denom[:, :]))
            dve.tensor_tensor(gate[:, 1, :], egap[:, :], gate[:, 0, :], ALU.mult).then_inc(s_gate, 1)

            def split_picked(st):
                wait(dve, C.xhi, st.value + 1)
                width, blocks = C.width(st), st.blocks()
                dve.tensor_copy(back[:, bass.ds(st.value, 1), 0:blocks].rearrange("p t r -> p (t r)"),
                                picked[:, st.parity, 0:blocks, P:P + 1].bitcast(I32).rearrange("p r w -> p (r w)"))
                dve.tensor_tensor(xs[:, st.parity, 1, 0:width], dx[:, 0:width],
                                  xs[:, st.parity, 0, 0:width].bitcast(F32), ALU.subtract).then_inc(C.xlo, 1)

            def step_c(st):
                if (st - 2).within(TILES):
                    done = st - 2
                    wait(dve, C.turned, done.value + 1)
                    wait(dve, s_zfree, done.value + 1)
                    blocks = done.blocks()
                    dve.tensor_copy(rows[:, done.parity, 0:blocks, :], tr[:, 0:blocks, :]).then_inc(C.rows, 1)
                if st.within(TILES):
                    if (st + 1).within(TILES):
                        split_picked(st + 1)
                    dve_hidden(dve, C, st, 0)
                if (st - 1).within(TILES):
                    wait(dve, C.down, st.value)
                    wait(dve, C.turned, st.value - 1)
                    width = C.width(st - 1)
                    dve.tensor_copy(yT[:, 0:width], dn[:, 0:width]).then_inc(C.flat, 1)
                if st.within(TILES):
                    dve_hidden(dve, C, st, 1)

            split_picked(Step(0, 0))
            run_tiles(dve, step_c)

            dve.wait_ge(s_xrows, 16)

            def finish(g):
                dve.wait_ge(s_z[g], 16 * TOPK)
                z0 = z_rows[:, g, 0, :].rearrange("p (s d) -> p s d", d=P)
                for r in range(FIN_GROUP):
                    s = g * FIN_GROUP + r
                    ins = dve.scalar_tensor_tensor(z0[:, r, :], z0[:, r, :], gate[:, 0, s:s + 1], x_rows[:, s, :],
                                                   ALU.mult, ALU.add)
                ins.then_inc(s_half, 1)

            for g in range(GROUPS):
                finish(g)

        @block_ctx.tensor
        def _(pe):
            def step_a(st):
                if st.is_step(1):
                    setup()
                if st.within(CHUNKS):
                    wait(pe, A.xlo, st.value + 1)
                    pe_up(pe, A, st, 0, fc1)
                if (st - 2).within(CHUNKS):
                    c = (st - 2).value
                    wait(pe, A.flat, c + 1)
                    wait(pe, A.flat2, c + 1)
                    wait(pe, A.rows2, c)
                    for r in range(RPT):
                        mm = pe.transpose(tr[:, r, :], yT[:, r * P:(r + 1) * P], ident[:, :])
                    mm.then_inc(A.turned, 1)
                    for r in range(RPT):
                        mm = pe.matmul(misc[:, r * EXP:(r + 1) * EXP], yT[:, r * P:(r + 1) * P],
                                       router[:, :], start=True, stop=True)
                    mm.then_inc(A.score, 1)
                prev = st - 1

                def down(g, last, between=None):
                    if prev.within(CHUNKS):
                        u = prev.parity
                        pe_down(pe, A, prev, g,
                                [(dn[0:SHARED, :], lambda w, f: fc2[:, w, f, :]),
                                 (dx[:, :], lambda w, f: cexp[:, u, w, f, :, :].rearrange("p r c -> p (r c)"))],
                                last, between)

                if prev.within(CHUNKS):
                    wait(pe, s_clo, st.value)
                    wait(pe, A.flat, st.value - 1)
                    wait(pe, A.flat2, st.value - 1)
                def rank():
                    wait(pe, s_either, st.value - 1)
                    pairs = either[:, :, :].rearrange("p r e -> p (r e)")
                    pe.matmul(misc[:, MISC_RANK:MISC_RANK + RPT * EXP], before[:, :], pairs,
                              start=True, stop=True)
                    pe.matmul(misc[:, MISC_TOTAL:MISC_TOTAL + RPT * EXP], ones_b[:, :], pairs,
                              start=True, stop=True).then_inc(s_ranked, 1)

                if st.within(CHUNKS):
                    down(0, False)
                    if (st - 2).within(CHUNKS):
                        rank()
                    pe_up(pe, A, st, 1, fc1)
                    down(1, True)
                else:
                    down(0, False, between=rank)
                    if not prev.within(CHUNKS):
                        rank()
                    down(1, True)

            def setup():
                pe.wait_ge(s_load[6], 16)
                pe.wait_ge(s_hot, 1)
                pe.matmul(misc[SHARED:P, 0:SEQS], cexp_bias[:, :], seq_hot[:, :], start=True, stop=True)\
                  .then_inc(s_bias, 1)
                pe.wait_ge(s_load[7], 16)
                pe.wait_ge(s_const, 17)
                pe.wait_ge(s_fc_lo, 2)

            pe.wait_ge(s_fc_lo, 1)
            run_steps(pe, CHUNKS, step_a)

            def transpose_picked(st):
                u = st.parity
                wait(pe, s_pick[u], 16 * (st.half + 1))
                wait(pe, C.xlo, st.value)
                for r in range(st.blocks()):
                    mm = pe.transpose(dx[:, r * P:(r + 1) * P], picked[:, u, r, 0:P], ident[:, :])
                mm.then_inc(C.tin, 1)

            def step_c(st):
                if st.within(TILES):
                    wait(pe, C.xlo, st.value + 1)
                    wait(pe, s_w1[st.parity], 16 * (st.half + 1))
                    pe_up(pe, C, st, 0, w1[:, st.parity, :, :])
                if (st + 1).within(TILES):
                    transpose_picked(st + 1)
                if (st - 2).within(TILES):
                    c = (st - 2).value
                    wait(pe, C.flat, c + 1)
                    for r in range((st - 2).blocks()):
                        mm = pe.transpose(tr[:, r, :], yT[:, r * P:(r + 1) * P], ident[:, :])
                    mm.then_inc(C.turned, 1)
                prev = st - 1

                def down(g, last):
                    if prev.within(TILES):
                        u = prev.parity
                        pe_down(pe, C, prev, g, [(dn[:, 0:C.width(prev)], lambda w, f: w2[:, u, w, f * P:(f + 1) * P])], last)

                if prev.within(TILES):
                    wait(pe, s_w2[prev.parity], 16 * (prev.half + 1))
                    wait(pe, C.flat, st.value - 1)
                down(0, False)
                if st.within(TILES):
                    pe_up(pe, C, st, 1, w1[:, st.parity, :, :])
                down(1, True)

            transpose_picked(Step(0, 0))
            run_tiles(pe, step_c)


def kernel(x, itok_B_0_15, L0_cond_fc1_w, L0_cond_fc1_b, L0_cond_fc2_w, L0_cond_fc2_b,
           L0_cond_experts_w, L0_cond_experts_b, L0_ffn_router_w, L0_ffn_expert_w1, L0_ffn_expert_w2):
    import numpy as np
    import concourse.bacc as bacc
    from concourse.bass_utils import run_bass_kernel_spmd

    x = np.ascontiguousarray(x)
    arrays = {
        "xT": x.reshape(TOKENS, P).T,
        "x": x,
        "itok": np.asarray(itok_B_0_15).reshape(1, SEQS),
        "fc1T": np.asarray(L0_cond_fc1_w).T,
        "fc1_b": np.asarray(L0_cond_fc1_b).reshape(FB, P).T,
        "fc2T": np.asarray(L0_cond_fc2_w).reshape(SHARED, FB, P).transpose(2, 1, 0),
        "fc2_b": np.asarray(L0_cond_fc2_b).reshape(SHARED, 1),
        "cexpT": np.asarray(L0_cond_experts_w).reshape(CEXP, PART, FB, P).transpose(0, 3, 2, 1)
                   .reshape(CEXP, P, FB * PART),
        "cexp_b": np.asarray(L0_cond_experts_b),
        "routerT": np.asarray(L0_ffn_router_w).T,
        "w1T": np.asarray(L0_ffn_expert_w1).transpose(2, 0, 1),
        "w2T": np.asarray(L0_ffn_expert_w2).reshape(EXP, P, FB, P).transpose(3, 0, 2, 1).reshape(P, EXP, HID),
    }
    arrays = {"in_" + k: np.ascontiguousarray(v) for k, v in arrays.items()}
    nc = bacc.Bacc("TRN2", target_bir_lowering=False, num_devices=1)
    args = [nc.dram_tensor(k, v.shape, mybir.dt.from_np(v.dtype), kind="ExternalInput").ap()
            for k, v in arrays.items()]
    out = nc.dram_tensor("out", (SEQS, P, P), F32, kind="ExternalOutput").ap()
    build(nc, *args, out)
    r = run_bass_kernel_spmd(nc, [arrays], core_ids=[0])
    return r.results[0]["out"]
```
